# Optimizing a Trainium2 kernel written in Bass

```python
import numpy as np
import jax
import jax.numpy as jnp

def _softmax(x, axis=-1):
    return jax.nn.softmax(x, axis=axis)

def _gelu(x):
    return jax.nn.gelu(x, approximate=True)

def _silu(x):
    return jax.nn.silu(x)

def _sigmoid(x):
    return jax.nn.sigmoid(x)

def _layernorm(x, axis=-1, eps=1e-05):
    m = jnp.mean(x, axis=axis, keepdims=True)
    v = jnp.var(x, axis=axis, keepdims=True)
    return (x - m) / jnp.sqrt(v + eps)

def _scatter_add(tgt, idx, src, axis=0):
    return tgt.at[idx].add(src)

def _segment_sum(src, seg, n):
    return jax.ops.segment_sum(src, seg, n)
kernel_name = 'mk_gnn_resnorm_d2_gnn_r8_d35c77'

def setup_inputs(seed: int=0):
    np.random.seed(seed)
    _w = jnp.asarray

    def _rec_inputs():
        import jax
        import jax.numpy as jnp
        _gk = jax.random.key(seed)
        x = -0.0005121 + 1.001 * jax.random.normal(jax.random.fold_in(_gk, 1), (12500, 128), jnp.float32)
        src = jax.random.randint(jax.random.fold_in(_gk, 2), (200000,), 0, 12500, jnp.int32)
        dst = jax.random.randint(jax.random.fold_in(_gk, 3), (200000,), 0, 12500, jnp.int32)
        _o = jnp.argsort(dst, stable=True)
        src = src[_o]
        dst = dst[_o]
        edge_attr_4 = -0.00166765 + 0.999426 * jax.random.normal(jax.random.fold_in(_gk, 12), (200000, 4), jnp.float32)
        edge_attr_8 = -0.00016606 + 0.999594 * jax.random.normal(jax.random.fold_in(_gk, 13), (200000, 8), jnp.float32)
        node_vec1 = 0.00192408 + 1.00201 * jax.random.normal(jax.random.fold_in(_gk, 15), (12500, 1), jnp.float32)
        node_vec1_n2 = 0.00192408 + 1.00201 * jax.random.normal(jax.random.fold_in(_gk, 16), (12500, 1), jnp.float32)
        return (x, src, dst, edge_attr_4, edge_attr_8, node_vec1, node_vec1_n2)
    x, src, dst, edge_attr_4, edge_attr_8, node_vec1, node_vec1_n2 = _rec_inputs()

    def _L0_gnn_setup():
        import jax, jax.numpy as jnp
        import numpy as np
        N = 3125
        E = 50000
        MUL = 32
        NSC = 8
        HID = 64
        WNUM = 4 * MUL
        NUM_NEIGH = 16.0
        INV_SQRT3 = 1.0 / np.sqrt(3.0)
        key = jax.random.key(seed)
        ks = jax.random.split(key, 13)
        return {'node_input': jax.random.normal(ks[0], (N, 4 * MUL), jnp.float32), 'node_attr_input': jax.random.normal(ks[1], (N, 1), jnp.float32), 'node_attr_output': jax.random.normal(ks[2], (N, 1), jnp.float32), 'edge_src': jax.random.randint(ks[3], (E,), 0, N), 'edge_dst': jax.random.randint(ks[4], (E,), 0, N), 'edge_attr': jax.random.normal(ks[5], (E, 4), jnp.float32), 'edge_scalar_attr': jax.random.normal(ks[6], (E, NSC), jnp.float32), 'w1_s': jax.random.normal(ks[7], (MUL, MUL), jnp.float32), 'w1_v': jax.random.normal(ks[8], (MUL, MUL), jnp.float32), 'Wfc1': jax.random.normal(ks[9], (NSC, HID), jnp.float32), 'Wfc2': jax.random.normal(ks[10], (HID, WNUM), jnp.float32), 'w2_s': jax.random.normal(ks[11], (2, MUL, MUL), jnp.float32), 'w2_v': jax.random.normal(ks[12], (2, MUL, MUL), jnp.float32)}
    _L0_gnn_all = _L0_gnn_setup()
    _L0_gnn_in = {k: v for k, v in _L0_gnn_all.items() if k in ('w1_s', 'w1_v', 'Wfc1', 'Wfc2', 'w2_s', 'w2_v')}
    del _L0_gnn_all

    def _L1_gnn_setup():
        import math
        import jax, jax.numpy as jnp
        import numpy as np
        N = 6250
        C = 128
        H = 8
        D = C // H
        E = 100000

        def _layernorm(x, g, b, eps=1e-05):
            mu = jnp.mean(x, axis=-1, keepdims=True)
            var = jnp.var(x, axis=-1, keepdims=True)
            return (x - mu) * jax.lax.rsqrt(var + eps) * g + b
        key = jax.random.key(seed)
        ks = jax.random.split(key, 12)
        s = 1.0 / math.sqrt(C)
        s4 = 1.0 / math.sqrt(4 * C)
        return {'x': jax.random.normal(ks[0], (N, C), dtype=jnp.float32), 'edge_index': jax.random.randint(ks[1], (2, E), 0, N, dtype=jnp.int64), 'Wq': jax.random.normal(ks[2], (C, C), dtype=jnp.float32) * s, 'Wk': jax.random.normal(ks[3], (C, C), dtype=jnp.float32) * s, 'Wv': jax.random.normal(ks[4], (C, C), dtype=jnp.float32) * s, 'Wo': jax.random.normal(ks[5], (C, C), dtype=jnp.float32) * s, 'bo': jnp.zeros((C,), dtype=jnp.float32), 'Wf1': jax.random.normal(ks[6], (C, 4 * C), dtype=jnp.float32) * s, 'bf1': jnp.zeros((4 * C,), dtype=jnp.float32), 'Wf2': jax.random.normal(ks[7], (4 * C, C), dtype=jnp.float32) * s4, 'bf2': jnp.zeros((C,), dtype=jnp.float32), 'g1': jnp.ones((C,), dtype=jnp.float32), 'b1': jnp.zeros((C,), dtype=jnp.float32), 'g2': jnp.ones((C,), dtype=jnp.float32), 'b2': jnp.zeros((C,), dtype=jnp.float32)}
    _L1_gnn_all = _L1_gnn_setup()
    _L1_gnn_in = {k: v for k, v in _L1_gnn_all.items() if k in ('Wq', 'Wk', 'Wv', 'Wo', 'bo', 'Wf1', 'bf1', 'Wf2', 'bf2', 'g1', 'b1', 'g2', 'b2')}
    del _L1_gnn_all
    return {'x': x, 'src': src, 'dst': dst, 'edge_attr_4': edge_attr_4, 'edge_attr_8': edge_attr_8, 'node_vec1': node_vec1, 'node_vec1_n2': node_vec1_n2, 'L0_gnn_w1_s': _L0_gnn_in['w1_s'], 'L0_gnn_w1_v': _L0_gnn_in['w1_v'], 'L0_gnn_Wfc1': _L0_gnn_in['Wfc1'], 'L0_gnn_Wfc2': _L0_gnn_in['Wfc2'], 'L0_gnn_w2_s': _L0_gnn_in['w2_s'], 'L0_gnn_w2_v': _L0_gnn_in['w2_v'], 'L1_gnn_Wq': _L1_gnn_in['Wq'], 'L1_gnn_Wk': _L1_gnn_in['Wk'], 'L1_gnn_Wv': _L1_gnn_in['Wv'], 'L1_gnn_Wo': _L1_gnn_in['Wo'], 'L1_gnn_bo': _L1_gnn_in['bo'], 'L1_gnn_Wf1': _L1_gnn_in['Wf1'], 'L1_gnn_bf1': _L1_gnn_in['bf1'], 'L1_gnn_Wf2': _L1_gnn_in['Wf2'], 'L1_gnn_bf2': _L1_gnn_in['bf2'], 'L1_gnn_g1': _L1_gnn_in['g1'], 'L1_gnn_b1': _L1_gnn_in['b1'], 'L1_gnn_g2': _L1_gnn_in['g2'], 'L1_gnn_b2': _L1_gnn_in['b2']}

def reference(x, src, dst, edge_attr_4, edge_attr_8, node_vec1, node_vec1_n2, L0_gnn_w1_s, L0_gnn_w1_v, L0_gnn_Wfc1, L0_gnn_Wfc2, L0_gnn_w2_s, L0_gnn_w2_v, L1_gnn_Wq, L1_gnn_Wk, L1_gnn_Wv, L1_gnn_Wo, L1_gnn_bo, L1_gnn_Wf1, L1_gnn_bf1, L1_gnn_Wf2, L1_gnn_bf2, L1_gnn_g1, L1_gnn_b1, L1_gnn_g2, L1_gnn_b2):
    import jax
    import jax.numpy as jnp

    def _L0_gnn_ref(node_input, node_attr_input, node_attr_output, edge_src, edge_dst, edge_attr, edge_scalar_attr, w1_s, w1_v, Wfc1, Wfc2, w2_s, w2_v):
        import jax, jax.numpy as jnp
        import numpy as np
        N = 3125
        E = 50000
        MUL = 32
        NSC = 8
        HID = 64
        WNUM = 4 * MUL
        NUM_NEIGH = 16.0
        INV_SQRT3 = 1.0 / np.sqrt(3.0)
        n = node_input.shape[0]
        xs = node_input[:, :MUL]
        xv = node_input[:, MUL:].reshape(n, MUL, 3)
        a = node_attr_input[:, 0]
        inv1 = 1.0 / np.sqrt(MUL * 1.0)
        xs1 = jnp.einsum('nu,n,uw->nw', xs, a, w1_s) * inv1
        xv1 = jnp.einsum('nui,n,uw->nwi', xv, a, w1_v) * inv1
        h = jax.nn.silu(edge_scalar_attr @ Wfc1 * (1.0 / np.sqrt(NSC)))
        w = (h @ Wfc2 * (1.0 / np.sqrt(HID))).reshape(-1, 4, MUL)
        es = xs1[edge_src]
        ev = xv1[edge_src]
        ys = edge_attr[:, 0]
        yv = edge_attr[:, 1:4]
        m0 = w[:, 0] * es * ys[:, None]
        m3 = w[:, 3] * jnp.einsum('eui,ei->eu', ev, yv) * INV_SQRT3
        m1 = w[:, 1][:, :, None] * es[:, :, None] * yv[:, None, :]
        m2 = w[:, 2][:, :, None] * ev * ys[:, None, None]
        ne = m0.shape[0]
        edge_features = jnp.concatenate([m0, m3, m1.reshape(ne, 3 * MUL), m2.reshape(ne, 3 * MUL)], axis=1)
        mid = jax.ops.segment_sum(edge_features, edge_dst, num_segments=n)
        mid = mid / np.sqrt(NUM_NEIGH)
        b = node_attr_output[:, 0]
        inv2 = 1.0 / np.sqrt(2.0 * MUL)
        s0 = mid[:, :MUL]
        s1 = mid[:, MUL:2 * MUL]
        v1 = mid[:, 2 * MUL:2 * MUL + 3 * MUL].reshape(n, MUL, 3)
        v2 = mid[:, 2 * MUL + 3 * MUL:].reshape(n, MUL, 3)
        out_s = (jnp.einsum('nu,n,uw->nw', s0, b, w2_s[0]) + jnp.einsum('nu,n,uw->nw', s1, b, w2_s[1])) * inv2
        out_v = (jnp.einsum('nui,n,uw->nwi', v1, b, w2_v[0]) + jnp.einsum('nui,n,uw->nwi', v2, b, w2_v[1])) * inv2
        return jnp.concatenate([out_s, out_v.reshape(n, 3 * MUL)], axis=1)

    def _L1_gnn_ref(x, edge_index, Wq, Wk, Wv, Wo, bo, Wf1, bf1, Wf2, bf2, g1, b1, g2, b2):
        import math
        import jax, jax.numpy as jnp
        import numpy as np
        N = 6250
        C = 128
        H = 8
        D = C // H
        E = 100000

        def _layernorm(x, g, b, eps=1e-05):
            mu = jnp.mean(x, axis=-1, keepdims=True)
            var = jnp.var(x, axis=-1, keepdims=True)
            return (x - mu) * jax.lax.rsqrt(var + eps) * g + b
        n = x.shape[0]
        loops = jnp.arange(n, dtype=edge_index.dtype)
        row = jnp.concatenate([edge_index[0], loops])
        col = jnp.concatenate([edge_index[1], loops])
        q = (x @ Wq).reshape(n, H, D)
        k = (x @ Wk).reshape(n, H, D)
        v = (x @ Wv).reshape(n, H, D)
        scores = jnp.einsum('ehd,ehd->eh', q[row], k[col]) / math.sqrt(D)
        smax = jax.ops.segment_max(scores, col, num_segments=n)
        exp = jnp.exp(scores - smax[col])
        ssum = jax.ops.segment_sum(exp, col, num_segments=n)
        alpha = exp / (ssum[col] + 1e-08)
        out = jax.ops.segment_sum(v[row] * alpha[..., None], col, num_segments=n)
        attn = out.reshape(n, C) @ Wo + bo
        residual = x
        x1 = _layernorm(residual + attn, g1, b1)
        ffn = jax.nn.gelu(x1 @ Wf1 + bf1, approximate=False) @ Wf2 + bf2
        return _layernorm(x1 + ffn, g2, b2)
    edge_index = jnp.stack([src, dst])
    x = _layernorm(x + _L0_gnn_ref(x, node_vec1, node_vec1_n2, src, dst, edge_attr_4, edge_attr_8, L0_gnn_w1_s, L0_gnn_w1_v, L0_gnn_Wfc1, L0_gnn_Wfc2, L0_gnn_w2_s, L0_gnn_w2_v), axis=-1)
    x = _layernorm(x + _L1_gnn_ref(x, edge_index, L1_gnn_Wq, L1_gnn_Wk, L1_gnn_Wv, L1_gnn_Wo, L1_gnn_bo, L1_gnn_Wf1, L1_gnn_bf1, L1_gnn_Wf2, L1_gnn_bf2, L1_gnn_g1, L1_gnn_b1, L1_gnn_g2, L1_gnn_b2), axis=-1)
    return x

_drawn_inputs = setup_inputs


def setup_inputs(seed=0):
    import zlib

    import numpy as np

    out = dict(_drawn_inputs(seed))
    spreads = {'L1_gnn_bo': (0.0, 0.1),
     'L1_gnn_bf1': (0.0, 0.275),
     'L1_gnn_bf2': (0.0, 0.1),
     'L1_gnn_g1': (1.0, 0.2),
     'L1_gnn_b1': (0.0, 0.1),
     'L1_gnn_g2': (1.0, 0.2),
     'L1_gnn_b2': (0.0, 0.1)}
    factors = {}
    for name, (base, spread) in spreads.items():
        noise = np.random.default_rng([zlib.crc32(name.encode()), seed]).standard_normal(out[name].shape)
        drawn = base * np.exp(spread * noise) if base else spread * noise
        out[name] = jnp.asarray(drawn.astype(out[name].dtype))
    for name, factor in factors.items():
        out[name] = (out[name] * factor).astype(out[name].dtype)
    return out
```

```python
from contextlib import ExitStack

import concourse.bass as bass
from concourse import mybir

F32 = mybir.dt.float32
I32 = mybir.dt.int32
ALU = mybir.AluOpType
ACT = mybir.ActivationFunctionType
AX = mybir.AxisListType

P = 128
N_NODES, N_EDGES, C = 12500, 200000, 128
NB = -(-N_NODES // P)
NP = NB * P
HALF = 16
T = -(-N_EDGES // (P * HALF)) * HALF
EP = T * P
NH = T // HALF
TP, TC = 112, T // 112
LEAD = 2 * P
MUL, HID, HEADS, HD, FF = 32, 64, 8, 16, 512
W0 = 8 * MUL
W1 = C + 2 * HEADS
AUX = P + 1
CH = 7
NCH = NB // CH
BIG = 1.0e30
EPS = 1e-5
INV1 = 1.0 / MUL ** 0.5
INV2 = 1.0 / (2.0 * MUL) ** 0.5
INV_SQRT3 = 1.0 / 3.0 ** 0.5
CONV_SCALE = INV2 / 16.0 ** 0.5 / HID ** 0.5


class Shared:
    pass


class Chain:

    def __init__(self, eng, sem):
        self.eng, self.sem, self.n = eng, sem, 0

    def __call__(self, ins):
        self.n += 1
        ins.then_inc(self.sem, 1)
        self.eng.wait_ge(self.sem, self.n)


def hold(eng, sem, value, passed):
    eng.wait_ge(sem, value)
    eng.sem_inc(passed, 1)


def scope(nc, ctx):
    made = []
    def sb(name, shape, dt=F32):
        return ctx.enter_context(nc.sbuf_tensor(name, shape, dt))

    def pb(name, shape, dt=F32):
        return ctx.enter_context(nc.psum_tensor(name, shape, dt))

    def sem(name):
        made.append(nc.alloc_semaphore(name))
        return made[-1]

    def clear():
        nc.all_engine_barrier()
        nc.clear_and_free_semaphores(made)
        nc.all_engine_barrier()

    ctx.callback(clear)
    return sb, pb, sem


def prepare(nc, g, a):
    with ExitStack() as ctx:
        sb, pb, sem = scope(nc, ctx)
        dst_t = sb("dst_t", [P, T], I32)
        prev_t = sb("prev_t", [P, T], I32)
        start_t = sb("start_t", [P, T])
        dst_b = sb("dst_b", [TP, TC, P], I32)
        prev_b = sb("prev_b", [TP, TC, P], I32)
        next_b = sb("next_b", [TP, TC, P], I32)
        neg_start = sb("neg_start", [TP, TC, P])
        neg_end = sb("neg_end", [TP, TC, P])
        around = sb("around", [TP, 3, TC], I32)
        first = sb("first", [TP, TC])
        first_hi = sb("first_hi", [TP, TC], I32)
        first_lo = sb("first_lo", [TP, TC], I32)
        first_hif = sb("first_hif", [TP, TC])
        first_lof = sb("first_lof", [TP, TC])
        cont = sb("cont", [TP, 5, TC])
        keep = sb("keep", [TP, TC])
        tile_no = sb("tile_no", [TP, TC])
        chain_idx = g.chain_idx
        lo_lt = sb("lo_lt", [TP, TC, P])
        hi_eq = sb("hi_eq", [TP, TC, NB])
        hi_lt = sb("hi_lt", [TP, TC, NB])
        tri = sb("tri", [P, P])
        tri_s = sb("tri_s", [P, P])
        up1 = sb("up1", [P, P])
        wrap1 = sb("wrap1", [P, P])
        ones = sb("ones", [P, P])
        ones_row = sb("ones_row", [1, T])
        totals = sb("totals", [1, T])
        incl = sb("incl", [1, T])
        last_tile = sb("last_tile", [P, NB])
        last_idx = sb("last_idx", [P, NB], I32)
        gidx = sb("gidx", [P, 2, TC], I32)
        aux = sb("aux", [P, 2, TC * AUX], I32)
        less = sb("less", [P, TC, P])
        node = sb("node", [P, NB], I32)
        nodef = sb("nodef", [P, NB])
        before = sb("before", [P, NB])
        rank_of = sb("rank_of", [P, NB])
        edge0 = sb("edge0", [P, NB + 1])
        edge1 = sb("edge1", [P, NB])
        some = sb("some", [P, NB])
        cum = sb("cum", [P, NB])
        cum_x = sb("cum_x", [P, NB])
        run = sb("run", [P, NB])
        tmp = sb("tmp", [P, 4, NB])
        fill = sb("fill", [P, W0])
        fill1 = sb("fill1", [P, W1])
        xt = sb("xt", [P, 2, CH * P])
        f0 = sb("f0", [P, 2, CH, C])
        a_s = sb("a_s", [P, NB])
        ps = pb("ps_prep", [P, 8, 512])

        loaded = sem("p_loaded")
        weights = sem("p_weights")
        xt_in = [sem(f"p_xt{i}") for i in range(2)]
        f0_out = [sem(f"p_f0{i}") for i in range(2)]
        consts = sem("p_consts")
        dve = sem("p_dve")
        pool = sem("p_pool")
        start_ok = sem("p_start")
        ranked = sem("p_ranked")
        rel_ok = sem("p_rel")
        totals_ok = sem("p_totals")
        rank0_ok = sem("p_rank0")
        aux_out = sem("p_auxout")
        neg_ok = sem("p_neg")
        keep_ok = sem("p_keep")
        hist_in = sem("p_histin")
        hist_ok = sem("p_hist")
        idx_ok = sem("p_idx")
        aux_in = [sem(f"p_aux{i}") for i in range(2)]
        aux_used = sem("p_auxused")
        edge0_ok = sem("p_edge0")
        edge1_ok = sem("p_edge1")
        cum_ok = sem("p_cum")
        run_ok = sem("p_run")
        fill_ok = sem("p_fill")
        w_ok = sem("p_w")
        a_ok = sem("p_a")
        f0_mm = sem("p_f0mm")
        f0_ev = sem("p_f0ev")
        stored = sem("p_stored")
        stores = [0]
        block = ctx.enter_context(nc.Block())

        flat = lambda off: a["dst_flat"][LEAD + off:LEAD + off + EP].rearrange("(p c e) -> p c e", c=TC, e=P)
        nodes_of = lambda table, c: table.rearrange("(h p) w -> p h w", p=P)[:, CH * c:CH * c + CH, :]
        f0_v = g.f0.rearrange("(h p) w -> p h w", p=P)

        @block.sync
        def _(sp):
            def store(dst, src, **how):
                sp.dma_start(dst, src, **how).then_inc(stored, 16)
                stores[0] += 16

            sp.dma_start(dst_t[:, :], a["dst_t"]).then_inc(loaded, 16)
            sp.dma_start(prev_t[:, :], a["prev_t"]).then_inc(loaded, 16)
            sp.dma_start(dst_b[:, :, :], flat(0)).then_inc(loaded, 16)
            sp.dma_start(prev_b[:, :, :], flat(-1)).then_inc(loaded, 16)
            sp.dma_start(next_b[:, :, :], flat(1)).then_inc(loaded, 16)
            sp.dma_start(around[:, :, :], a["around"]).then_inc(loaded, 16)
            sp.wait_ge(w_ok, 1)
            sp.dma_start(g.w_node[0:MUL, 0:MUL], a["w1_s"]).then_inc(weights, 16)
            for i in range(3):
                sp.dma_start(g.w_node[MUL + i:P:3, MUL * (1 + i):MUL * (2 + i)], a["w1_v"]).then_inc(weights, 16)
            for q in range(4):
                for h in range(2):
                    sp.dma_start(g.w_hidden[32 * q + 8 * h:32 * q + 8 * h + 8, HID * h:HID * h + HID],
                                 a["wfc1"]).then_inc(weights, 16)
            for h in range(2):
                sp.dma_start(g.w_mix[HID * h:HID * h + HID, h, :], a["wfc2"]).then_inc(weights, 16)
            for m, rows in enumerate(((a["w2_s"][0], a["w2_s"][1], a["w2_v"][0], a["w2_v"][0]),
                                      (a["w2_v"][0], a["w2_v"][1], a["w2_v"][1], a["w2_v"][1]))):
                for q, src in enumerate(rows):
                    sp.dma_start(g.w_after_in[32 * q:32 * q + 32, m, :], src).then_inc(weights, 16)
            sp.dma_start(g.w_qvk[:, 0:C], a["wq"]).then_inc(weights, 16)
            sp.dma_start(g.w_qvk[:, C:2 * C], a["wv"]).then_inc(weights, 16)
            sp.dma_start(g.w_qvk[:, 2 * C:3 * C], a["wk"]).then_inc(weights, 16)
            sp.dma_start(a_s[:, :], a["a_in"]).then_inc(weights, 16)
            sp.dma_start(g.b_scale[:, :], a["b_in"]).then_inc(weights, 16)
            sp.dma_start(g.y[:, :, :], a["edge4"]).then_inc(weights, 16)
            def load_xt(c):
                sp.dma_start(xt[:, c % 2, :], a["x_t"][:, c * CH * P:(c + 1) * CH * P]).then_inc(xt_in[c % 2], 16)

            load_xt(0)
            load_xt(1)
            sp.wait_ge(loaded, 96)
            store(g.aux[:, 0:P].rearrange("(p c) e -> p c e", c=TC), dst_b[:, :, :])
            sp.wait_ge(rank0_ok, 1)
            store(g.aux[:, P:P + 1], g.rank0[0:1, :], allow_slow_non_contiguous=True)
            sp.wait_ge(stored, stores[0])
            sp.nop().then_inc(aux_out, 1)
            sp.wait_ge(neg_ok, 2)
            for m, src in enumerate((neg_start, neg_end)):
                for h in range(HEADS):
                    store(g.resets[:, h, m, :].rearrange("(p c) e -> p c e", c=TC), src[:, :, :])
            sp.wait_ge(keep_ok, 1)
            store(g.keep.rearrange("(p c) -> p c", c=TC), keep[:, :])
            sp.wait_ge(fill_ok, 1)
            store(g.sums0[EP:EP + P, :], fill[:, :])
            store(g.sums1[EP:EP + P, :], fill1[:, :])
            store(g.k_runs[NP:NP + P, :], fill[:, 0:C])
            for h0 in range(0, NB, CH):
                store(g.chains0[P * h0:P * (h0 + CH), :].rearrange("(h p) w -> p h w", p=P),
                      fill[:, :].unsqueeze(1).broadcast_to([P, CH, W0]))
                store(g.chains1[P * h0:P * (h0 + CH), :].rearrange("(h p) w -> p h w", p=P),
                      fill1[:, :].unsqueeze(1).broadcast_to([P, CH, W1]))
            for c in range(NCH):
                sp.wait_ge(f0_ev, (c + 1) * CH)
                sp.dma_start(f0_v[:, CH * c:CH * c + CH, :], f0[:, c % 2, :, :]).then_inc(f0_out[c % 2], 16)
                if c + 2 < NCH:
                    load_xt(c + 2)
            sp.wait_ge(stored, stores[0])
            for i in range(2):
                sp.wait_ge(f0_out[i], 16 * NCH // 2)

        @block.gpsimd
        def _(gp):
            link = Chain(gp, pool)
            gp.memset(ones[:, :], 1.0)
            gp.memset(ones_row[:, :], 1.0)
            gp.memset(fill[:, :], 0.0)
            gp.memset(fill1[:, 0:C + HEADS], 0.0)
            gp.memset(fill1[:, C + HEADS:W1], -BIG)
            link(gp.memset(g.ident[:, :], 0.0))
            gp.nop().then_inc(fill_ok, 1)
            gp.affine_select(out=g.ident[:, :], in_=g.ident[:, :], compare_op=ALU.not_equal, fill=1.0, base=0,
                             pattern=[[-1, P]], channel_multiplier=1)
            gp.iota(g.column[:, :], pattern=[[1, P]], base=0, channel_multiplier=0,
                    allow_small_or_imprecise_dtypes=True)
            gp.iota(node[:, :], pattern=[[P, NB]], base=0, channel_multiplier=1)
            gp.iota(nodef[:, :], pattern=[[P, NB]], base=0, channel_multiplier=1,
                    allow_small_or_imprecise_dtypes=True)
            gp.iota(tile_no[:, :], pattern=[[1, TC]], base=NP, channel_multiplier=TC,
                    allow_small_or_imprecise_dtypes=True)
            link(gp.affine_select(out=tri[:, :], in_=ones[:, :], compare_op=ALU.is_ge, fill=0.0, base=0,
                                  pattern=[[1, P]], channel_multiplier=-1))
            link(gp.affine_select(out=tri[:, :], in_=tri[:, :], compare_op=ALU.is_ge, fill=0.0, base=-1,
                                  pattern=[[0, P]], channel_multiplier=1))
            link(gp.affine_select(out=tri_s[:, :], in_=ones[:, :], compare_op=ALU.is_ge, fill=0.0, base=-1,
                                  pattern=[[1, P]], channel_multiplier=-1))
            link(gp.memset(up1[:, :], 0.0))
            link(gp.memset(wrap1[:, :], 0.0))
            link(gp.affine_select(out=up1[:, :], in_=up1[:, :], compare_op=ALU.not_equal, fill=1.0, base=-1,
                                  pattern=[[-1, P]], channel_multiplier=1))
            link(gp.affine_select(out=wrap1[:, :], in_=wrap1[:, :], compare_op=ALU.not_equal, fill=1.0, base=P - 1,
                                  pattern=[[-1, P]], channel_multiplier=P))
            gp.nop().then_inc(consts, 1)
            gp.wait_ge(idx_ok, 1)
            gp.wait_ge(aux_out, 1)
            for r in range(NCH // 2):
                if r >= 2:
                    gp.wait_ge(aux_used, r - 1)
                for k in range(TC):
                    gp.indirect_dma_start(aux[:, r % 2, k * AUX:(k + 1) * AUX], None, g.aux,
                                          bass.IndirectOffsetOnAxis(ap=last_idx[:, TC * r + k:TC * r + k + 1], axis=0)
                                          ).then_inc(aux_in[r % 2], 16)

        @block.vector
        def _(v):
            link = Chain(v, dve)
            v.memset(g.w_node[:, :], 0.0)
            v.memset(g.w_mix[:, :, :], 0.0)
            v.memset(g.w_hidden[:, :], 0.0).then_inc(w_ok, 1)
            link(v.memset(g.w_after[:, :, :], 0.0))
            v.wait_ge(weights, 16 * 28)
            comp = lambda i: g.w_after[:, :, MUL:C].rearrange("p m (w i) -> p m i w", i=3)[:, :, i, :]
            v.tensor_copy(g.w_after[0:32, 0, 0:MUL], g.w_after_in[0:32, 0, :])
            v.tensor_scalar(g.w_after[32:64, 0, 0:MUL], g.w_after_in[32:64, 0, :], INV_SQRT3, None, ALU.mult)
            for m, q, i in ((0, 2, 0), (0, 3, 1), (1, 0, 2), (1, 1, 0), (1, 2, 1), (1, 3, 2)):
                v.tensor_copy(comp(i)[32 * q:32 * q + 32, m, :], g.w_after_in[32 * q:32 * q + 32, m, :])
            v.tensor_scalar(g.b_scale[:, :], g.b_scale[:, :], CONV_SCALE, None, ALU.mult)
            v.tensor_scalar(a_s[:, :], a_s[:, :], INV1, None, ALU.mult).then_inc(a_ok, 1)
            v.wait_ge(loaded, 96)
            v.wait_ge(consts, 1)
            v.tensor_tensor(start_t[:, :], dst_t[:, :], prev_t[:, :], ALU.not_equal).then_inc(start_ok, 1)
            link(v.tensor_single_scalar(first_hi[:, :], dst_b[:, :, 0], 7, ALU.logical_shift_right))
            link(v.tensor_single_scalar(first_lo[:, :], dst_b[:, :, 0], P - 1, ALU.bitwise_and))
            v.tensor_copy(first_hif[:, :], first_hi[:, :])
            v.tensor_copy(first[:, :], dst_b[:, :, 0])
            link(v.tensor_copy(first_lof[:, :], first_lo[:, :]))
            for c in range(TC):
                v.tensor_scalar(lo_lt[:, c, :], g.column[0:TP, :], first_lof[:, c:c + 1], None, ALU.is_gt)
                v.tensor_scalar(hi_eq[:, c, :], g.column[0:TP, 0:NB], first_hif[:, c:c + 1], None, ALU.is_equal)
                v.tensor_scalar(hi_lt[:, c, :], g.column[0:TP, 0:NB], first_hif[:, c:c + 1], None,
                                ALU.is_gt).then_inc(hist_in, 1)
            for k in range(4):
                v.wait_ge(ranked, k + 1)
                v.tensor_copy(g.rel[:, k * 392:(k + 1) * 392], ps[:, k, 0:392]).then_inc(rel_ok, 1)
            for k in range(4):
                v.wait_ge(totals_ok, k + 1)
                link(v.tensor_copy(totals[0:1, k * 392:(k + 1) * 392], ps[0:1, 4 + k, 0:392]))
            link(v.tensor_tensor_scan(incl[:, :], ones_row[:, :], totals[:, :], 0.0, ALU.mult, ALU.add))
            link(v.tensor_tensor(incl[:, :], incl[:, :], totals[:, :], ALU.subtract))
            v.scalar_tensor_tensor(g.rank0[:, :], incl[:, :], -1.0, start_t[0:1, :], ALU.add,
                                   ALU.add).then_inc(rank0_ok, 1)
            for out, other in ((neg_start, prev_b), (neg_end, next_b)):
                link(v.tensor_tensor(out[:, :, :], dst_b[:, :, :], other[:, :, :], ALU.not_equal))
                ins = v.tensor_scalar(out[:, :, :], out[:, :, :], -BIG, None, ALU.mult)
                if out is neg_start:
                    ins.then_inc(neg_ok, 1)
            link(ins)
            v.memset(neg_end[:, :, P - 1:P], -BIG).then_inc(neg_ok, 1)
            v.tensor_tensor(cont[:, 0, :], dst_b[:, :, 0], prev_b[:, :, 0], ALU.is_equal)
            v.tensor_tensor(cont[:, 1, :], around[:, 0, :], around[:, 1, :], ALU.is_equal)
            v.tensor_tensor(cont[:, 2, :], around[:, 0, :], dst_b[:, :, 0], ALU.is_equal)
            v.tensor_tensor(cont[:, 3, :], around[:, 2, :], dst_b[:, :, P - 1], ALU.is_equal)
            link(v.tensor_tensor(cont[:, 4, :], around[:, 2, :], dst_b[:, :, 0], ALU.is_equal))
            link(v.tensor_tensor(cont[:, 1, :], cont[:, 1, :], cont[:, 2, :], ALU.mult))
            v.tensor_tensor(keep[:, :], cont[:, 1, :], cont[:, 0, :], ALU.mult).then_inc(keep_ok, 1)
            link(v.tensor_tensor(cont[:, 3, :], cont[:, 3, :], cont[:, 4, :], ALU.mult))
            link(v.tensor_tensor(cont[:, 3, :], cont[:, 0, :], cont[:, 3, :], ALU.is_gt))
            link(v.tensor_tensor(cont[:, 0, :], first[:, :], tile_no[:, :], ALU.subtract))
            link(v.tensor_tensor(cont[:, 0, :], cont[:, 0, :], cont[:, 3, :], ALU.mult))
            link(v.tensor_tensor(chain_idx[:, :], cont[:, 0, :], tile_no[:, :], ALU.add))
            v.wait_ge(hist_ok, 1)
            link(v.tensor_scalar(last_tile[:, :], ps[:, 0, 0:NB], -1.0, 0.0, ALU.add, ALU.max))
            v.tensor_copy(last_idx[:, :], last_tile[:, :]).then_inc(idx_ok, 1)
            for r in range(NCH // 2):
                v.wait_ge(aux_in[r % 2], 16 * TC * (r // 2 + 1))
                rows = aux[:, r % 2, :].rearrange("p (k w) -> p k w", w=AUX)
                cols = slice(TC * r, TC * r + TC)
                link(v.tensor_tensor(less[:, :, :], rows[:, :, 0:P],
                                     node[:, cols].unsqueeze(2).broadcast_to([P, TC, P]), ALU.is_lt))
                link(v.tensor_reduce(before[:, cols], less[:, :, :], AX.X, ALU.add))
                v.tensor_copy(rank_of[:, cols], rows[:, :, P]).then_inc(aux_used, 1)
            v.memset(edge0[:, NB:NB + 1], float(EP))
            link(v.memset(cum_x[:, 0:1], 0.0))
            v.scalar_tensor_tensor(edge0[:, 0:NB], last_tile[:, :], float(P), before[:, :], ALU.mult,
                                   ALU.add).then_inc(edge0_ok, 1)
            v.wait_ge(edge0_ok, 1)
            v.wait_ge(edge1_ok, 1)
            link(v.tensor_tensor(some[:, :], ps[:, 1, 0:NB], edge0[:, 0:NB], ALU.is_gt))
            link(v.tensor_tensor_scan(cum[:, :], ones[:, 0:NB], some[:, :], 0.0, ALU.mult, ALU.add))
            v.tensor_copy(cum_x[:, 1:NB], cum[:, 0:NB - 1]).then_inc(cum_ok, 1)
            v.wait_ge(run_ok, 1)
            link(v.tensor_copy(run[:, :], ps[:, 2, 0:NB]))
            link(v.tensor_tensor(tmp[:, 0, :], nodef[:, :], run[:, :], ALU.subtract))
            link(v.tensor_scalar(tmp[:, 0, :], tmp[:, 0, :], ps[:, 3, 0:1], None, ALU.add))
            link(v.tensor_tensor(tmp[:, 1, :], run[:, :], tmp[:, 0, :], ALU.subtract))
            link(v.tensor_tensor(tmp[:, 1, :], tmp[:, 1, :], some[:, :], ALU.mult))
            link(v.tensor_tensor(g.k_idx[:, :], tmp[:, 1, :], tmp[:, 0, :], ALU.add))
            link(v.tensor_scalar(tmp[:, 0, :], before[:, :], float(P), None, ALU.is_equal))
            link(v.tensor_tensor(tmp[:, 1, :], run[:, :], rank_of[:, :], ALU.subtract))
            link(v.tensor_tensor(tmp[:, 2, :], tmp[:, 1, :], tmp[:, 0, :], ALU.mult))
            link(v.tensor_tensor(tmp[:, 1, :], tmp[:, 1, :], tmp[:, 2, :], ALU.subtract))
            link(v.tensor_tensor(tmp[:, 0, :], last_tile[:, :], tmp[:, 0, :], ALU.add))
            link(v.scalar_tensor_tensor(tmp[:, 0, :], tmp[:, 0, :], float(P), tmp[:, 1, :], ALU.mult, ALU.add))
            link(v.scalar_tensor_tensor(tmp[:, 0, :], tmp[:, 0, :], -float(EP), some[:, :], ALU.add, ALU.mult))
            link(v.tensor_scalar(g.sum_idx[:, :], tmp[:, 0, :], float(EP), None, ALU.add))

        @block.scalar
        def _(act):
            act.wait_ge(a_ok, 1)
            for c in range(NCH):
                if c >= 2:
                    act.wait_ge(f0_out[c % 2], 16 * (c // 2))
                for k in range(CH):
                    b = CH * c + k
                    act.wait_ge(f0_mm, b + 1)
                    nc.scalar.activation(f0[:, c % 2, k, :], ps[:, 4 + b % 4, 0:C], ACT.Copy,
                                         scale=a_s[:, b:b + 1]).then_inc(f0_ev, 1)

        @block.tensor
        def _(pe):
            pe.wait_ge(consts, 1)
            pe.wait_ge(start_ok, 1)
            for k in range(4):
                nc.tensor.matmul(ps[:, k, 0:392], tri[:, :], start_t[:, k * 392:(k + 1) * 392],
                                 start=True, stop=True).then_inc(ranked, 1)
            for k in range(4):
                nc.tensor.matmul(ps[0:1, 4 + k, 0:392], ones[:, 0:1], start_t[:, k * 392:(k + 1) * 392],
                                 start=True, stop=True).then_inc(totals_ok, 1)
            pe.wait_ge(rel_ok, 4)
            for c in range(TC):
                pe.wait_ge(hist_in, c + 1)
                nc.tensor.matmul(ps[:, 0, 0:NB], lo_lt[:, c, :], hi_eq[:, c, :], start=(c == 0), stop=False)
                last = nc.tensor.matmul(ps[:, 0, 0:NB], ones[0:TP, :], hi_lt[:, c, :], start=False,
                                        stop=(c == TC - 1))
            last.then_inc(hist_ok, 1)
            pe.wait_ge(weights, 16 * 28)
            pe.wait_ge(rank0_ok, 1)
            for c in range(NCH):
                pe.wait_ge(xt_in[c % 2], 16 * (c // 2 + 1))
                for k in range(CH):
                    b = CH * c + k
                    if b >= 4:
                        pe.wait_ge(f0_ev, b - 3)
                    nc.tensor.matmul(ps[:, 4 + b % 4, 0:C], xt[:, c % 2, k * P:(k + 1) * P], g.w_node[:, :],
                                     start=True, stop=True).then_inc(f0_mm, 1)
            pe.wait_ge(edge0_ok, 1)
            nc.tensor.matmul(ps[:, 1, 0:NB], up1[:, :], edge0[:, 0:NB], start=True, stop=False)
            nc.tensor.matmul(ps[:, 1, 0:NB], wrap1[:, :], edge0[:, 1:NB + 1], start=False,
                             stop=True).then_inc(edge1_ok, 1)
            pe.wait_ge(cum_ok, 1)
            nc.tensor.matmul(ps[:, 2, 0:NB], tri_s[:, :], some[:, :], start=True, stop=False)
            nc.tensor.matmul(ps[:, 2, 0:NB], ones[:, :], cum_x[:, :], start=False, stop=True)
            nc.tensor.matmul(ps[:, 3, 0:1], ones[:, :], cum[:, NB - 1:NB], start=True,
                             stop=True).then_inc(run_ok, 1)


def edge_convolution(nc, g, a):
    with ExitStack() as ctx:
        sb, pb, sem = scope(nc, ctx)
        QT = 4
        NG = T // QT
        U = 8
        idx = sb("c_idx", [P, 2, HALF], I32)
        attr = sb("c_attr", [P, 2, 2 * P])
        x_src = sb("c_x", [P, 4, QT, C])
        hid = sb("c_hid", [P, 2, 2 * P])
        hot = sb("c_hot", [P, 2, QT, P])
        msg = sb("c_msg", [P, 2, QT, W0])
        we = sb("c_we", [P, QT, 2 * MUL])
        wy = sb("c_wy", [P, QT, MUL])
        vy = sb("c_vy", [P, QT, 3 * MUL])
        dot = sb("c_dot", [P, QT, MUL])
        out = sb("c_out", [P, 2, QT, W0])
        ps_h = [pb(f"c_ps_h{i}", [P, 512]) for i in range(2)]
        ps_w = [pb(f"c_ps_w{i}", [P, QT, P]) for i in range(2)]
        ps_s = [[pb(f"c_ps_s{i}{j}", [P, 512]) for j in range(2)] for i in range(2)]

        idx_in = [sem(f"c_idx_in{i}") for i in range(2)]
        attr_in = [sem(f"c_attr_in{i}") for i in range(2)]
        gathered = [sem(f"c_gathered{i}") for i in range(4)]
        stored = [sem(f"c_stored{i}") for i in range(2)]
        hidden = sem("c_hidden")
        silu_ok = sem("c_silu")
        mixed = sem("c_mixed")
        hot_ok = sem("c_hot_ok")
        dve = sem("c_dve")
        msg_ok = sem("c_msg_ok")
        summed = sem("c_summed")
        staged = sem("c_staged")
        passed = sem("c_passed")
        block = ctx.enter_context(nc.Block())

        table = g.sums0[0:EP, :].rearrange("(t r) w -> r t w", r=P)

        def groups(eng, step):
            for u in range(U):
                step(0, u)
            with eng.Fori(1, NG // U - 1) as i:
                for u in range(U):
                    step(i, u)
            for u in range(U):
                step(NG // U - 1, u)

        def early(i, u, n):
            return isinstance(i, int) and U * i + u < n

        def late(i, u, n):
            return isinstance(i, int) and U * i + u >= NG - n

        @block.sync
        def _(sp):
            def load(i, h):
                if not (isinstance(i, int) and i == 0):
                    hold(sp, hidden, i * U + 4 * h - 4, passed)
                    for q in range(4):
                        hold(sp, gathered[q], 16 * QT * (2 * i + h - 1), passed)
                sp.dma_start(attr[:, h, :], a["edge8_t"][bass.ds(i * 2 + h, 1), :, :].rearrange("o p n -> p (o n)")
                             ).then_inc(attr_in[h], 16)
                sp.dma_start(idx[:, h, :], a["src_t"][bass.ds(i * 2 + h, 1), :, :].rearrange("o p n -> p (o n)")
                             ).then_inc(idx_in[h], 16)

            def store(i, u):
                j = i * U + u
                hold(sp, staged, j + 1, passed)
                sp.dma_start(table[:, bass.ds(j * QT, QT), :], out[:, u % 2, :, :]).then_inc(stored[u % 2], 16)

            load(0, 0)
            load(0, 1)
            for u in range(U):
                store(0, u)
                if u % 4 == 3:
                    load(1, u // 4)
            with sp.Fori(1, NG // U - 1) as i:
                for u in range(U):
                    store(i, u)
                    if u % 4 == 3:
                        load(i + 1, u // 4)
            for u in range(U):
                store(NG // U - 1, u)
            for b in range(2):
                sp.wait_ge(stored[b], 16 * NG // 2)

        @block.gpsimd
        def _(gp):
            def step(i, u):
                h = u // 4
                if u % 4 == 0:
                    hold(gp, idx_in[h], 16 * (i + 1), passed)
                if not early(i, u, 4):
                    hold(gp, msg_ok, i * U + (u - 3), passed)
                for k in range(QT):
                    c = QT * (u % 4) + k
                    gp.indirect_dma_start(x_src[:, u % 4, k, :], None, g.f0,
                                          bass.IndirectOffsetOnAxis(ap=idx[:, h, c:c + 1], axis=0)
                                          ).then_inc(gathered[u % 4], 16)
            groups(gp, step)

        @block.scalar
        def _(act):
            def silu(i, u):
                act.wait_ge(hidden, i * U + u + 1)
                if not early(i, u, 2):
                    act.wait_ge(mixed, i * U + (u - 1))
                nc.scalar.activation(hid[:, u % 2, :], ps_h[u % 2][:, 0:2 * P], ACT.Silu,
                                     scale=1.0 / HEADS ** 0.5).then_inc(silu_ok, 1)

            def stage(i, u):
                act.wait_ge(summed, i * U + u + 1)
                if not early(i, u, 2):
                    act.wait_ge(stored[u % 2], 16 * (4 * i + (u - 2) // 2 + 1))
                for m in range(2):
                    last = nc.scalar.activation(out[:, u % 2, 2 * m:2 * m + 2, :],
                                                ps_s[u % 2][m][:, :].rearrange("p (k w) -> p k w", k=2), ACT.Copy)
                last.then_inc(staged, 1)

            def step(i, u):
                if not late(i, u, 1):
                    if u + 1 < U:
                        silu(i, u + 1)
                    else:
                        silu(i + 1, 0)
                if not early(i, u, 1):
                    if u:
                        stage(i, u - 1)
                    else:
                        stage(i - 1, U - 1)

            silu(0, 0)
            groups(act, step)
            stage(NG // U - 1, U - 1)

        @block.vector
        def _(v):
            STEPS = 8

            def step(i, u):
                j = i * U + u
                b = u % 2
                w = ps_w[b][:, :, :].rearrange("p k (m c) -> p k m c", m=4)
                x = x_src[:, u % 4, :, :].rearrange("p k (m c) -> p k m c", m=4)
                y = g.y[:, bass.ds(j * QT, QT), :]
                y0 = y[:, :, 0:1].broadcast_to([P, QT, MUL])
                y3 = y[:, :, 1:4].unsqueeze(3).broadcast_to([P, QT, 3, MUL])
                o = msg[:, b, :, :]
                done = [0]

                def sig(ins):
                    ins.then_inc(dve, 1)
                    done[0] += 1
                    return done[0]

                def after(n):
                    v.wait_ge(dve, j * STEPS + n)

                if not early(i, u, 2):
                    v.wait_ge(summed, j - 1)
                for k in range(QT):
                    last = v.tensor_scalar(hot[:, b, k, :], g.column[:, :], g.rel[:, bass.ds(j * QT + k, 1)], None,
                                           ALU.is_equal)
                last.then_inc(hot_ok, 1)
                v.wait_ge(gathered[u % 4], 16 * QT * (2 * i + u // 4 + 1))
                n_vy = sig(v.tensor_tensor(vy[:, :, :].rearrange("p k (m c) -> p k m c", m=3), x[:, :, 1:4, :], y3,
                                           ALU.mult))
                v.wait_ge(mixed, j + 1)
                n_we = sig(v.tensor_tensor(we[:, :, :].rearrange("p k (m c) -> p k m c", m=2), w[:, :, 0:2, :],
                                           x[:, :, 0:1, :].broadcast_to([P, QT, 2, MUL]), ALU.mult))
                n_wy = sig(v.tensor_tensor(wy[:, :, :], w[:, :, 2, :], y0, ALU.mult))
                after(n_vy)
                n_d = sig(v.tensor_tensor(dot[:, :, :], vy[:, :, 0:MUL], vy[:, :, MUL:2 * MUL], ALU.add))
                after(n_we)
                n_m0 = sig(v.tensor_tensor(o[:, :, 0:MUL], we[:, :, 0:MUL], y0, ALU.mult))
                v.tensor_tensor(o[:, :, 2 * MUL:5 * MUL].rearrange("p k (m c) -> p k m c", m=3),
                                we[:, :, MUL:2 * MUL].unsqueeze(2).broadcast_to([P, QT, 3, MUL]), y3, ALU.mult)
                after(n_d)
                n_d2 = sig(v.tensor_tensor(dot[:, :, :], dot[:, :, :], vy[:, :, 2 * MUL:3 * MUL], ALU.add))
                after(n_wy)
                n_m2 = sig(v.tensor_tensor(o[:, :, 5 * MUL:8 * MUL].rearrange("p k (m c) -> p k m c", m=3),
                                           wy[:, :, :].unsqueeze(2).broadcast_to([P, QT, 3, MUL]), x[:, :, 1:4, :],
                                           ALU.mult))
                after(n_d2)
                n_m3 = sig(v.tensor_tensor(o[:, :, MUL:2 * MUL], w[:, :, 3, :], dot[:, :, :], ALU.mult))
                assert done[0] == STEPS
                after(n_m3)
                v.nop().then_inc(msg_ok, 1)
            groups(v, step)

        @block.tensor
        def _(pe):
            def first_layer(i, u):
                if u % 4 == 0:
                    pe.wait_ge(attr_in[u // 4], 16 * (i + 1))
                if not early(i, u, 2):
                    pe.wait_ge(silu_ok, i * U + (u - 1))
                q = 32 * (u % 4)
                nc.tensor.matmul(ps_h[u % 2][:, 0:2 * P], g.w_hidden[q:q + 16, :], attr[q:q + 16, u // 4, :],
                                 start=True, stop=True).then_inc(hidden, 1)

            def second_layer(i, u):
                pe.wait_ge(silu_ok, i * U + u + 1)
                if not early(i, u, 2):
                    pe.wait_ge(msg_ok, i * U + (u - 1))
                for pair in range(2):
                    last = nc.tensor.matmul(ps_w[u % 2][:, 2 * pair:2 * pair + 2, :],
                                            hid[:, u % 2, P * pair:P * pair + P], g.w_mix[:, :, :],
                                            start=True, stop=True)
                last.then_inc(mixed, 1)

            def sums(i, u):
                pe.wait_ge(hot_ok, i * U + u + 1)
                pe.wait_ge(msg_ok, i * U + u + 1)
                if not early(i, u, 2):
                    pe.wait_ge(staged, i * U + (u - 1))
                for k in range(QT):
                    last = nc.tensor.matmul(ps_s[u % 2][k // 2][:, W0 * (k % 2):W0 * (k % 2) + W0],
                                            hot[:, u % 2, k, :], msg[:, u % 2, k, :], start=True, stop=True)
                last.then_inc(summed, 1)

            def step(i, u):
                second_layer(i, u)
                if not late(i, u, 1):
                    if u + 1 < U:
                        first_layer(i, u + 1)
                    else:
                        first_layer(i + 1, 0)
                if not early(i, u, 1):
                    if u:
                        sums(i, u - 1)
                    else:
                        sums(i - 1, U - 1)

            first_layer(0, 0)
            groups(pe, step)
            sums(NG // U - 1, U - 1)


def chain_sums(nc, g, rows, table, width, name, heads):
    with ExitStack() as ctx:
        sb, pb, sem = scope(nc, ctx)
        NQ = T // 4
        row_in = sb(name + "row", [TP, TC, width])
        row_out = sb(name + "out", [TP, TC, width])
        keep = sb(name + "keep", [P, T])
        parts = [(0, C), (C, 2 * C)] if not heads else [(0, C), (C, C + HEADS), (C + HEADS, width)]
        turned = [sb(f"{name}t{i}", [b - a, T]) for i, (a, b) in enumerate(parts)]
        total = [sb(f"{name}s{i}", [b - a, T]) for i, (a, b) in enumerate(parts)]
        if heads:
            reset = sb(name + "reset", [HEADS, T + 1])
            spread = sb(name + "spread", [HEADS, C])
            weight = sb(name + "weight", [HEADS, T])
        ps = pb(name + "ps", [P, 8, 512])
        loaded = sem(name + "loaded")
        pe_ok = sem(name + "pe")
        ev_ok = sem(name + "ev")
        total_ok = sem(name + "total")
        back_ok = sem(name + "back")
        row_ok = sem(name + "rowok")
        scattered = sem(name + "scattered")
        dve = sem(name + "dve")
        weighed = sem(name + "weighed")
        diff_ok = sem(name + "diff")
        spread_ok = sem(name + "spread")
        wide_ok = sem(name + "wide")
        wide_used = sem(name + "wideused")
        block = ctx.enter_context(nc.Block())
        jobs = [(c, i) for i in reversed(range(len(parts))) for c in range(TC)]

        @block.sync
        def _(sp):
            sp.dma_start(row_in[:, :, :],
                         rows[0:EP, :].rearrange("(p c r) w -> p c r w", c=TC, r=P)[:, :, 0, :]).then_inc(loaded, 16)
            sp.dma_start(keep[:, :], g.keep.unsqueeze(0).broadcast_to([P, T])).then_inc(loaded, 16)

        @block.tensor
        def _(pe):
            pe.wait_ge(loaded, 32)
            for n, (c, i) in enumerate(jobs):
                lo, hi = parts[i]
                if n >= 4:
                    pe.wait_ge(ev_ok, n - 3)
                nc.tensor.transpose(ps[0:hi - lo, n % 4, 0:TP], row_in[:, c, lo:hi],
                                    g.ident[0:TP, 0:TP]).then_inc(pe_ok, 1)
            if heads:
                pe.wait_ge(weighed, 1)
                pe.wait_ge(spread_ok, 1)
                pe.wait_ge(ev_ok, len(jobs))
                for k in range(4):
                    nc.tensor.matmul(ps[:, k, 0:NQ], spread[:, :], weight[:, k * NQ:(k + 1) * NQ], start=True,
                                     stop=True).then_inc(wide_ok, 1)
            pe.wait_ge(total_ok, 1)
            for n, (c, i) in enumerate(jobs):
                lo, hi = parts[i]
                if n >= 4:
                    pe.wait_ge(row_ok, n - 3)
                nc.tensor.transpose(ps[0:TP, 4 + n % 4, 0:hi - lo],
                                    total[i][:, :].rearrange("w (p c) -> w c p", c=TC)[:, c, :],
                                    g.ident[0:hi - lo, 0:hi - lo]).then_inc(back_ok, 1)

        @block.scalar
        def _(act):
            for n, (c, i) in enumerate(jobs):
                lo, hi = parts[i]
                act.wait_ge(pe_ok, n + 1)
                nc.scalar.activation(turned[i][:, :].rearrange("w (p c) -> w c p", c=TC)[:, c, :],
                                     ps[0:hi - lo, n % 4, 0:TP], ACT.Copy).then_inc(ev_ok, 1)
            if heads:
                act.wait_ge(diff_ok, 1)
                nc.scalar.activation(weight[:, :], weight[:, :], ACT.Exp).then_inc(weighed, 1)
            for n, (c, i) in enumerate(jobs):
                lo, hi = parts[i]
                act.wait_ge(back_ok, n + 1)
                nc.scalar.activation(row_out[:, c, lo:hi], ps[0:TP, 4 + n % 4, 0:hi - lo],
                                     ACT.Copy).then_inc(row_ok, 1)

        @block.vector
        def _(v):
            link = Chain(v, dve)
            v.wait_ge(loaded, 32)
            v.wait_ge(ev_ok, len(jobs))
            if heads:
                acc, den, top = turned
                link(v.tensor_scalar(reset[:, 0:T], keep[0:HEADS, :], -1.0, BIG, ALU.add, ALU.mult))
                link(v.memset(reset[:, T:T + 1], -BIG))
                link(v.tensor_tensor_scan(weight[:, :], reset[:, 0:T], top[:, :], -BIG, ALU.add, ALU.max))
                link(v.tensor_tensor_scan(total[2][:, ::-1], reset[:, 1:T + 1][:, ::-1], weight[:, ::-1], -BIG,
                                          ALU.add, ALU.max))
                link(v.tensor_tensor(weight[:, :], top[:, :], total[2][:, :], ALU.subtract))
                v.nop().then_inc(diff_ok, 1)
                v.wait_ge(weighed, 1)
                link(v.tensor_tensor(den[:, :], den[:, :], weight[:, :], ALU.mult))
                for k in range(4):
                    v.wait_ge(wide_ok, k + 1)
                    link(v.tensor_tensor(acc[:, k * NQ:(k + 1) * NQ], acc[:, k * NQ:(k + 1) * NQ],
                                         ps[:, k, 0:NQ], ALU.mult))
            for i in range(2):
                link(v.tensor_tensor_scan(total[i][:, :], keep[0:turned[i].shape[0], :], turned[i][:, :], 0.0,
                                          ALU.mult, ALU.add))
            v.nop().then_inc(total_ok, 1)

        @block.gpsimd
        def _(gp):
            if heads:
                gp.memset(spread[:, :], 1.0).then_inc(wide_used, 1)
                gp.wait_ge(wide_used, 1)
                gp.affine_select(out=spread[:, :], in_=spread[:, :], compare_op=ALU.is_ge, fill=0.0, base=0,
                                 pattern=[[1, C]], channel_multiplier=-HD).then_inc(wide_used, 1)
                gp.wait_ge(wide_used, 2)
                gp.affine_select(out=spread[:, :], in_=spread[:, :], compare_op=ALU.is_ge, fill=0.0, base=HD - 1,
                                 pattern=[[-1, C]], channel_multiplier=HD).then_inc(spread_ok, 1)
            for c in range(TC):
                gp.wait_ge(row_ok, len(jobs) - TC + c + 1)
                gp.indirect_dma_start(table, bass.IndirectOffsetOnAxis(ap=g.chain_idx[:, c:c + 1], axis=0),
                                      row_out[:, c, :], None).then_inc(scattered, 16)
            gp.wait_ge(scattered, 16 * TC)


class Norm:

    def __init__(self, sb, sem, name):
        self.raw = sb(name + "raw", [P, CH, 6])
        self.stat = sb(name + "stat", [P, CH, 2])
        self.rstd = sb(name + "rstd", [P, CH])
        self.stats_ok = sem(name + "stats")
        self.rstd_ok = sem(name + "rstdok")
        self.passed = sem(name + "passed")

    def stats(self, v, link, x, n):
        for k in range(CH):
            v.bn_stats(self.raw[:, k, :], x[:, k, :]).then_inc(link.sem, 1)
            link.n += 1
        hold(v, link.sem, link.at(), self.passed)
        for k in range(CH):
            last = v.bn_aggr(self.stat[:, k, :], self.raw[:, k, :])
        last.then_inc(self.stats_ok, 1)

    def root(self, gp, link, half, n):
        hold(gp, self.stats_ok, n, self.passed)
        link(gp.tensor_scalar(self.rstd[:, :], self.stat[:, :, 1], EPS, None, ALU.add))
        gp.tensor_tensor(self.rstd[:, :], self.rstd[:, :], half[:, :], ALU.pow).then_inc(self.rstd_ok, 1)

    def apply(self, v, link, out, x, n):
        v.wait_ge(self.rstd_ok, n)
        for k in range(CH):
            last = v.tensor_scalar(out[:, k, :], x[:, k, :], self.stat[:, k, 0:1], self.rstd[:, k:k + 1],
                                   ALU.subtract, ALU.mult)
        link(last)


class Steps:

    def __init__(self, eng, sem, per, passed=None):
        self.eng, self.sem, self.per, self.n, self.base, self.passed = eng, sem, per, 0, 0, passed

    def round(self, c):
        assert self.n in (0, self.per), self.n
        self.base, self.n = c * self.per, 0

    def at(self):
        return self.base + self.n

    def __call__(self, ins):
        self.n += 1
        ins.then_inc(self.sem, 1)
        if self.passed is None:
            self.eng.wait_ge(self.sem, self.base + self.n)
        else:
            hold(self.eng, self.sem, self.base + self.n, self.passed)


def chunks(eng, step):
    step(0)
    with eng.Fori(1, NCH) as c:
        step(c)


def first_round(c):
    return isinstance(c, int)


def finish_convolution(nc, g, a):
    with ExitStack() as ctx:
        sb, pb, sem = scope(nc, ctx)
        idx = sb("d_idx", [P, 2, CH], I32)
        own = sb("d_own", [P, CH, W0])
        chain = sb("d_chain", [P, CH, W0])
        x_in = sb("d_x", [P, CH, C])
        mid_t = sb("d_mid_t", [P, CH, 2, P])
        pre = sb("d_pre", [P, CH, C])
        x1 = sb("d_x1", [P, CH, C])
        x1_t = sb("d_x1_t", [P, CH, P])
        qvk = sb("d_qvk", [P, CH, 3 * C])
        keys = sb("d_keys", [P, CH, C])
        prod = sb("d_prod", [P, CH, C])
        half = sb("d_half", [P, CH])
        ps_t = [pb(f"d_ps_t{i}", [P, 4, P]) for i in range(2)]
        ps_o = pb("d_ps_o", [P, 8, C])
        ps_q = [pb(f"d_ps_q{i}", [P, 512]) for i in range(4)]
        norm = Norm(sb, sem, "d_n")
        x_ok = sem("d_x_in")
        chain_ok = sem("d_chain_in")
        own_ok = sem("d_own_in")
        idx_ok = sem("d_idx_ok")
        mid_ok = sem("d_mid")
        t_ok = sem("d_t")
        t_ev = sem("d_tev")
        out_ok = sem("d_out")
        x1_ok = sem("d_x1ok")
        q_ok = sem("d_q")
        q_ev = sem("d_qev")
        keys_ok = sem("d_keysok")
        self_ok = sem("d_self")
        stored = [sem(f"d_stored{i}") for i in range(2)]
        scattered = sem("d_scattered")
        dve = sem("d_dve")
        pool = sem("d_pool")
        passed = sem("d_passed")
        block = ctx.enter_context(nc.Block())
        rows = lambda t, c: t[0:NP, :].rearrange("(h p) w -> p h w", p=P)[:, bass.ds(c * CH, CH), :]
        MID = [(0, 4), (4, 8), (8, 12), (12, 14)]
        ONE = [(0, 4), (4, 7)]

        @block.sync
        def _(sp):
            def step(c):
                if not first_round(c):
                    hold(sp, x1_ok, c, passed)
                sp.dma_start(x_in[:, :, :], rows(a["x_rows"], c)).then_inc(x_ok, 16)
                sp.dma_start(chain[:, :, :], rows(g.chains0, c)).then_inc(chain_ok, 16)
                hold(sp, x1_ok, c + 1, passed)
                sp.dma_start(rows(g.x1, c), x1[:, :, :]).then_inc(stored[0], 16)
                hold(sp, q_ev, (c + 1) * CH, passed)
                sp.dma_start(rows(g.qv, c), qvk[:, :, 0:2 * C]).then_inc(stored[1], 16)
            chunks(sp, step)
            for i in range(2):
                sp.wait_ge(stored[i], 16 * NCH)

        @block.gpsimd
        def _(gp):
            link = Steps(gp, pool, 3, passed)
            gp.memset(half[:, :], -0.5)

            def step(c):
                link.round(c)
                if not first_round(c):
                    hold(gp, scattered, 16 * CH * c, passed)
                link(gp.tensor_copy(idx[:, 0, :], g.sum_idx[:, bass.ds(c * CH, CH)]))
                link(gp.tensor_copy(idx[:, 1, :], g.k_idx[:, bass.ds(c * CH, CH)]))
                if not first_round(c):
                    hold(gp, mid_ok, c, passed)
                for k in range(CH):
                    gp.indirect_dma_start(own[:, k, :], None, g.sums0,
                                          bass.IndirectOffsetOnAxis(ap=idx[:, 0, k:k + 1], axis=0)
                                          ).then_inc(own_ok, 16)
                norm.root(gp, link, half, c + 1)
                hold(gp, keys_ok, c + 1, passed)
                for k in range(CH):
                    gp.indirect_dma_start(g.k_runs, bass.IndirectOffsetOnAxis(ap=idx[:, 1, k:k + 1], axis=0),
                                          keys[:, k, :], None).then_inc(scattered, 16)
            chunks(gp, step)
            gp.wait_ge(scattered, 16 * CH * NCH)

        @block.vector
        def _(v):
            link = Steps(v, dve, CH + 4)

            def step(c):
                link.round(c)
                v.wait_ge(own_ok, 16 * CH * (c + 1))
                v.wait_ge(chain_ok, 16 * (c + 1))
                link(v.tensor_tensor(own[:, :, :], own[:, :, :], chain[:, :, :], ALU.add))
                v.nop().then_inc(mid_ok, 1)
                v.wait_ge(out_ok, c + 1)
                v.wait_ge(x_ok, 16 * (c + 1))
                for k in range(CH):
                    last = v.scalar_tensor_tensor(pre[:, k, :], ps_o[:, k, :], g.b_scale[:, bass.ds(c * CH + k, 1)],
                                                  x_in[:, k, :], ALU.mult, ALU.add)
                link(last)
                norm.stats(v, link, pre, c)
                if not first_round(c):
                    v.wait_ge(stored[0], 16 * c)
                norm.apply(v, link, x1, pre, c + 1)
                v.nop().then_inc(x1_ok, 1)
                v.wait_ge(q_ev, CH * (c + 1))
                if not first_round(c):
                    v.wait_ge(scattered, 16 * CH * c)
                link(v.tensor_scalar(keys[:, :, :], qvk[:, :, 2 * C:3 * C], 1.0 / HD ** 0.5, None, ALU.mult))
                v.nop().then_inc(keys_ok, 1)
                v.tensor_tensor(prod[:, :, :], keys[:, :, :], qvk[:, :, 0:C], ALU.mult).then_inc(self_ok, 1)
                v.wait_ge(self_ok, 2 * c + 1)
                v.tensor_reduce(g.self_score[:, bass.ds(c * CH, CH), :],
                                prod[:, :, :].rearrange("p k (h d) -> p k h d", d=HD), AX.X,
                                ALU.add).then_inc(self_ok, 1)
                v.wait_ge(self_ok, 2 * c + 2)
            chunks(v, step)

        @block.scalar
        def _(act):
            def step(c):
                for n, (lo, hi) in enumerate(MID):
                    act.wait_ge(t_ok, 6 * c + n + 1)
                    nc.scalar.activation(mid_t[:, :, :, :].rearrange("p k m n -> p (k m) n")[:, lo:hi, :],
                                         ps_t[n % 2][:, 0:hi - lo, :], ACT.Copy).then_inc(t_ev, 1)
                for n, (lo, hi) in enumerate(ONE):
                    act.wait_ge(t_ok, 6 * c + 5 + n)
                    nc.scalar.activation(x1_t[:, lo:hi, :], ps_t[n % 2][:, 0:hi - lo, :], ACT.Copy).then_inc(t_ev, 1)
                if not first_round(c):
                    act.wait_ge(stored[1], 16 * c)
                    act.wait_ge(self_ok, 2 * c)
                for k in range(CH):
                    act.wait_ge(q_ok, CH * c + k + 1)
                    nc.scalar.activation(qvk[:, k, :], ps_q[k % 4][:, 0:3 * C], ACT.Copy).then_inc(q_ev, 1)
            chunks(act, step)

        @block.tensor
        def _(pe):
            def step(c):
                pe.wait_ge(mid_ok, c + 1)
                own_v = own[:, :, :].rearrange("p k (m w) -> p (k m) w", m=2)
                for n, (lo, hi) in enumerate(MID + ONE):
                    if not (first_round(c) and n < 2):
                        pe.wait_ge(t_ev, 6 * c + n - 1)
                    if n == 4:
                        pe.wait_ge(t_ev, 6 * c + 4)
                        for k in range(CH):
                            for m in range(2):
                                last = nc.tensor.matmul(ps_o[:, k, :], mid_t[:, k, m, :], g.w_after[:, m, :],
                                                        start=(m == 0), stop=(m == 1))
                        last.then_inc(out_ok, 1)
                        pe.wait_ge(x1_ok, c + 1)
                    src = own_v if n < 4 else x1
                    for k in range(lo, hi):
                        last = nc.tensor.transpose(ps_t[n % 2][:, k - lo, :], src[:, k, :], g.ident[:, :])
                    last.then_inc(t_ok, 1)
                pe.wait_ge(t_ev, 6 * c + 6)
                for k in range(CH):
                    if first_round(c) and k < 4:
                        pass
                    else:
                        pe.wait_ge(q_ev, CH * c + k + 1 - 4)
                    nc.tensor.matmul(ps_q[k % 4][:, 0:3 * C], x1_t[:, k, :], g.w_qvk[:, :], start=True,
                                     stop=True).then_inc(q_ok, 1)
            chunks(pe, step)


def edge_attention(nc, g, a):
    with ExitStack() as ctx:
        sb, pb, sem = scope(nc, ctx)
        QT = 4
        NG = T // QT
        U = 8
        idx = sb("e_idx", [P, 2, HALF], I32)
        qv = sb("e_qv", [P, 2, HALF, 2 * C])
        keys = sb("e_keys", [P, 2, HALF, C])
        hot = sb("e_hot", [P, 2, HALF, P])
        hot_t = sb("e_hot_t", [P, 2, QT, P])
        prod = sb("e_prod", [P, QT, C])
        score = sb("e_score", [P, HALF * HEADS])
        reset = sb("e_reset", [P, 2, 2, P])
        fwd = sb("e_fwd", [P, P])
        top = sb("e_top", [P, P])
        diff = sb("e_diff", [P, P])
        top_end = sb("e_top_end", [P, P])
        prob = sb("e_prob", [P, P])
        rhs = sb("e_rhs", [P, 2, HALF, W1])
        out = sb("e_out", [P, 2, QT, W1])
        ps_t = [pb(f"e_ps_t{i}", [P, QT, P]) for i in range(2)]
        ps_k = [pb(f"e_ps_k{i}", [P, QT, C]) for i in range(2)]
        ps_s = pb("e_ps_s", [P, 512])
        ps_b = pb("e_ps_b", [P, 4, P])
        ps_o = [pb(f"e_ps_o{i}", [P, 512]) for i in range(2)]

        idx_in = [sem(f"e_idx_in{i}") for i in range(2)]
        reset_in = [sem(f"e_reset_in{i}") for i in range(2)]
        keys_in = [[sem(f"e_keys_in{i}{q}") for q in range(4)] for i in range(2)]
        gathered = [[sem(f"e_gathered{i}{q}") for q in range(4)] for i in range(2)]
        stored = [sem(f"e_stored{i}") for i in range(2)]
        hot_ok = sem("e_hot_ok")
        turned = sem("e_turned")
        hot_t_ok = sem("e_hot_t_ok")
        keyed = sem("e_keyed")
        multiplied = sem("e_multiplied")
        scored = sem("e_scored")
        score_turned = sem("e_score_turned")
        scans = sem("e_scans")
        diff_ok = sem("e_diff_ok")
        exp_ok = sem("e_exp")
        backed = sem("e_backed")
        copied = sem("e_copied")
        weighted = sem("e_weighted")
        summed = sem("e_summed")
        staged = sem("e_staged")
        passed = sem("e_passed")
        block = ctx.enter_context(nc.Block())
        table = g.sums1[0:EP, :].rearrange("(t r) w -> r t w", r=P)

        def groups(eng, step):
            for u in range(U):
                step(0, u)
            with eng.Fori(1, NG // U - 1) as i:
                for u in range(U):
                    step(i, u)
            for u in range(U):
                step(NG // U - 1, u)

        def early(i, u, n):
            return isinstance(i, int) and U * i + u < n

        def late(i, u, n):
            return isinstance(i, int) and U * i + u >= NG - n

        def ahead(i, u, n):
            return i + (u + n) // U, (u + n) % U

        @block.sync
        def _(sp):
            def load(i, u):
                h = u // 4
                if not early(i, u, U):
                    for q in range(4):
                        hold(sp, gathered[h][q], 16 * QT * i, passed)
                    hold(sp, diff_ok, 2 * i + h - 1, passed)
                    hold(sp, keyed, i * U + u - 4, passed)
                sp.dma_start(idx[:, h, :], a["src_t"][bass.ds(i * 2 + h, 1), :, :].rearrange("o p n -> p (o n)")
                             ).then_inc(idx_in[h], 16)
                sp.dma_start(reset[:, h, :, :],
                             g.resets[bass.ds((i * 2 + h) * HALF, HALF), :, :, :].rearrange("t h m e -> (t h) m e")
                             ).then_inc(reset_in[h], 16)
                for k in range(HALF):
                    t = (i * 2 + h) * HALF + k
                    row = sp.value_load(g.rank0[0:1, bass.ds(t, 1)], min_val=0, max_val=NP)
                    sp.dma_start(keys[:, h, k, :], g.k_runs[bass.ds(row, P), :]).then_inc(keys_in[h][k // QT], 16)

            def store(i, u):
                j = i * U + u
                hold(sp, staged, j + 1, passed)
                sp.dma_start(table[:, bass.ds(j * QT, QT), :], out[:, u % 2, :, :]).then_inc(stored[u % 2], 16)

            def step(i, u):
                if u % 4 == 0 and not late(i, u, 4):
                    load(*ahead(i, u, 4))
                if not early(i, u, 4):
                    store(*ahead(i, u, -4))

            load(0, 0)
            groups(sp, step)
            for u in range(4, U):
                store(NG // U - 1, u)
            for b in range(2):
                sp.wait_ge(stored[b], 16 * NG // 2)

        @block.gpsimd
        def _(gp):
            def step(i, u):
                h, q = u // 4, u % 4
                if q == 0:
                    hold(gp, idx_in[h], 16 * (i + 1), passed)
                if not early(i, u, U):
                    hold(gp, weighted, i * U + u - U + 1, passed)
                for k in range(QT):
                    c = QT * q + k
                    gp.indirect_dma_start(qv[:, h, c, :], None, g.qv,
                                          bass.IndirectOffsetOnAxis(ap=idx[:, h, c:c + 1], axis=0)
                                          ).then_inc(gathered[h][q], 16)
            groups(gp, step)

        @block.scalar
        def _(act):
            def copy_hot(i, u):
                j = i * U + u
                act.wait_ge(turned, j + 1)
                if not early(i, u, 2):
                    act.wait_ge(keyed, j - 1)
                nc.scalar.activation(hot_t[:, u % 2, :, :], ps_t[u % 2][:, :, :], ACT.Copy).then_inc(hot_t_ok, 1)

            def copy_back(i, u):
                h, n = u // 4, 2 * i + u // 4
                act.wait_ge(backed, n + 1)
                if not early(i, u, U):
                    act.wait_ge(summed, i * U + u - 4)
                nc.scalar.activation(rhs[:, h, :, C:W1].rearrange("p t (m x) -> p m t x", m=2),
                                     ps_b[:, 0:2, :].rearrange("p m (t x) -> p m t x", x=HEADS),
                                     ACT.Copy).then_inc(copied, 1)

            def stage(i, u):
                j = i * U + u
                act.wait_ge(summed, j + 1)
                if not early(i, u, 2):
                    act.wait_ge(stored[u % 2], 16 * (4 * i + (u - 2) // 2 + 1))
                for m in range(2):
                    last = nc.scalar.activation(out[:, u % 2, 2 * m:2 * m + 2, :],
                                                ps_o[m][:, 0:2 * W1].rearrange("p (k w) -> p k w", k=2), ACT.Copy)
                last.then_inc(staged, 1)

            def step(i, u):
                if not late(i, u, 1):
                    copy_hot(*ahead(i, u, 1))
                if not early(i, u, 4):
                    if u % 4 == 0:
                        copy_back(*ahead(i, u, -4))
                    stage(*ahead(i, u, -4))
                if u % 4 == 3:
                    n = 2 * i + u // 4
                    act.wait_ge(diff_ok, n + 1)
                    if not early(i, u, 4):
                        act.wait_ge(backed, n)
                    nc.scalar.activation(prob[:, :], diff[:, :], ACT.Exp).then_inc(exp_ok, 1)

            copy_hot(0, 0)
            groups(act, step)
            copy_back(NG // U - 1, 4)
            for u in range(4, U):
                stage(NG // U - 1, u)

        @block.vector
        def _(v):
            def one_hot(i, u):
                j, h, q = i * U + u, u // 4, u % 4
                if not early(i, u, U):
                    v.wait_ge(summed, j - U + 1)
                for k in range(QT):
                    last = v.tensor_scalar(hot[:, h, QT * q + k, :], g.column[:, :],
                                           g.rel[:, bass.ds(j * QT + k, 1)], None, ALU.is_equal)
                last.then_inc(hot_ok, 1)

            def weigh(i, u):
                h, q = u // 4, u % 4
                ts = slice(QT * q, QT * q + QT)
                if q == 0:
                    v.wait_ge(copied, 2 * i + h + 1)
                v.tensor_tensor(rhs[:, h, ts, 0:C].rearrange("p t (x d) -> p t x d", d=HD),
                                qv[:, h, ts, C:2 * C].rearrange("p t (x d) -> p t x d", d=HD),
                                rhs[:, h, ts, C:C + HEADS].unsqueeze(3).broadcast_to([P, QT, HEADS, HD]),
                                ALU.mult).then_inc(weighted, 1)

            def scores(i, u):
                j, h, q = i * U + u, u // 4, u % 4
                v.wait_ge(gathered[h][q], 16 * QT * (i + 1))
                v.wait_ge(keyed, j + 1)
                if not early(i, u, 1):
                    v.wait_ge(scored, j)
                v.tensor_tensor(prod[:, :, :], ps_k[u % 2][:, :, :], qv[:, h, QT * q:QT * q + QT, 0:C],
                                ALU.mult).then_inc(multiplied, 1)
                v.wait_ge(multiplied, j + 1)
                if q == 0 and not early(i, u, 4):
                    v.wait_ge(score_turned, 2 * i + h)
                v.tensor_reduce(score[:, QT * HEADS * q:QT * HEADS * (q + 1)],
                                prod[:, :, :].rearrange("p t (x d) -> p t x d", d=HD), AX.X,
                                ALU.add).then_inc(scored, 1)

            def maxima(i, u):
                h = u // 4
                n = 2 * i + h
                v.wait_ge(score_turned, n + 1)
                v.wait_ge(reset_in[h], 16 * (i + 1))
                v.tensor_tensor_scan(fwd[:, :], reset[:, h, 0, :], ps_s[:, 0:P], -BIG, ALU.add,
                                     ALU.max).then_inc(scans, 1)
                v.wait_ge(scans, 3 * n + 1)
                if not early(i, u, 4):
                    v.wait_ge(backed, n)
                v.tensor_tensor_scan(top[:, ::-1], reset[:, h, 1, ::-1], fwd[:, ::-1], -BIG, ALU.add,
                                     ALU.max).then_inc(scans, 1)
                v.wait_ge(scans, 3 * n + 2)
                v.scalar_tensor_tensor(top_end[:, :], reset[:, h, 1, :], 0.0, top[:, :], ALU.is_lt,
                                       ALU.mult).then_inc(scans, 1)
                v.tensor_tensor(diff[:, :], ps_s[:, 0:P], top[:, :], ALU.subtract).then_inc(diff_ok, 1)

            def step(i, u):
                q = u % 4
                if q != 3 and not late(i, u, 2):
                    one_hot(*ahead(i, u, 2))
                if q < 2 and not early(i, u, 4):
                    bi, bu = ahead(i, u, -4)
                    weigh(bi, bu + q)
                    weigh(bi, bu + q + 1)
                scores(i, u)
                if q == 3:
                    if not late(i, u, 2):
                        one_hot(*ahead(i, u, 2))
                    maxima(i, u)

            one_hot(0, 0)
            one_hot(0, 1)
            groups(v, step)
            for u in range(4, U):
                weigh(NG // U - 1, u)

        @block.tensor
        def _(pe):
            def turn(i, u):
                j, h, q = i * U + u, u // 4, u % 4
                pe.wait_ge(hot_ok, j + 1)
                if not early(i, u, 2):
                    pe.wait_ge(hot_t_ok, j - 1)
                for k in range(QT):
                    last = nc.tensor.transpose(ps_t[u % 2][:, k, :], hot[:, h, QT * q + k, :], g.ident[:, :])
                last.then_inc(turned, 1)

            def spread_keys(i, u):
                j, h, q = i * U + u, u // 4, u % 4
                pe.wait_ge(hot_t_ok, j + 1)
                pe.wait_ge(keys_in[h][q], 16 * QT * (i + 1))
                if not early(i, u, 2):
                    pe.wait_ge(multiplied, j - 1)
                for k in range(QT):
                    last = nc.tensor.matmul(ps_k[u % 2][:, k, :], hot_t[:, u % 2, k, :],
                                            keys[:, h, QT * q + k, :], start=True, stop=True)
                last.then_inc(keyed, 1)

            def back(i, u):
                n = 2 * i + u // 4
                pe.wait_ge(exp_ok, n + 1)
                if not early(i, u, 4):
                    pe.wait_ge(copied, n)
                nc.tensor.transpose(ps_b[:, 0, :], prob[:, :], g.ident[:, :])
                nc.tensor.transpose(ps_b[:, 1, :], top_end[:, :], g.ident[:, :]).then_inc(backed, 1)

            def sums(i, u):
                j, h, q = i * U + u, u // 4, u % 4
                pe.wait_ge(weighted, j + 1)
                if not early(i, u, 1):
                    pe.wait_ge(staged, j)
                for k in range(QT):
                    last = nc.tensor.matmul(ps_o[k // 2][:, W1 * (k % 2):W1 * (k % 2) + W1],
                                            hot[:, h, QT * q + k, :], rhs[:, h, QT * q + k, :],
                                            start=True, stop=True)
                last.then_inc(summed, 1)

            def step(i, u):
                if not late(i, u, 1):
                    turn(*ahead(i, u, 1))
                spread_keys(i, u)
                if not early(i, u, 4):
                    if u % 4 == 0:
                        back(*ahead(i, u, -4))
                    sums(*ahead(i, u, -4))
                if u % 4 == 3:
                    n = 2 * i + u // 4
                    pe.wait_ge(scored, i * U + u + 1)
                    if not early(i, u, 4):
                        pe.wait_ge(diff_ok, n)
                    nc.tensor.transpose(ps_s[:, 0:P], score[:, :], g.ident[:, :]).then_inc(score_turned, 1)

            turn(0, 0)
            groups(pe, step)
            back(NG // U - 1, 4)
            for u in range(4, U):
                sums(NG // U - 1, u)


def finish_attention(nc, g, a, out):
    with ExitStack() as ctx:
        sb, pb, sem = scope(nc, ctx)
        N = CH * P
        HH = N // 2
        wo = sb("f_wo", [P, C])
        wf1 = sb("f_wf1", [P, FF])
        wf2 = sb("f_wf2", [P, FF // P, C])
        bf1 = sb("f_bf1", [P, FF // P])
        vecs = sb("f_vecs", [P, 6, C])
        idx = sb("f_idx", [P, CH], I32)
        own = sb("f_own", [P, CH, W1])
        chain = sb("f_chain", [P, CH, W1])
        values = sb("f_values", [P, CH, C])
        x1 = sb("f_x1", [P, CH, C])
        top = sb("f_top", [P, CH, HEADS])
        part = sb("f_part", [P, 3, CH, HEADS])
        den = sb("f_den", [P, 2, CH, HEADS])
        acc = sb("f_acc", [P, CH, C])
        acc_t = sb("f_acc_t", [P, CH, P])
        pre = sb("f_pre", [P, CH, C])
        y1 = sb("f_y1", [P, CH, C])
        y1_t = sb("f_y1_t", [P, CH * P])
        hid = sb("f_hid", [P, FF // P, N])
        res = sb("f_res", [P, CH, C])
        half = sb("f_half", [P, CH])
        ps_t = [pb(f"f_ps_t{i}", [P, 4, P]) for i in range(2)]
        ps_o = pb("f_ps_o", [P, 8, C])
        ps_f = [pb(f"f_ps_f{i}", [P, 512]) for i in range(4)]
        norms = [Norm(sb, sem, f"f_n{i}") for i in range(3)]
        w_in = sem("f_w_in")
        ins_in = [sem(f"f_in{i}") for i in range(3)]
        own_ok = sem("f_own_ok")
        diff_ok = sem("f_diff")
        part_ok = sem("f_part_ok")
        acc_ok = sem("f_acc_ok")
        t_ok = sem("f_t")
        t_ev = sem("f_tev")
        o_ok = sem("f_o")
        y1_ok = sem("f_y1ok")
        h_ok = sem("f_h")
        h_ev = sem("f_hev")
        res_ok = sem("f_resok")
        stored = sem("f_stored")
        dve = sem("f_dve")
        pool = sem("f_pool")
        passed = sem("f_passed")
        block = ctx.enter_context(nc.Block())
        rows = lambda t, c: t[0:NP, :].rearrange("(h p) w -> p h w", p=P)[:, bass.ds(c * CH, CH), :]
        ONE = [(0, 4), (4, 7)]
        vec = lambda n: vecs[:, n:n + 1, :].broadcast_to([P, CH, C])
        wide = lambda t: t.unsqueeze(3).broadcast_to([P, CH, HEADS, HD])
        by_head = lambda t: t.rearrange("p k (x d) -> p k x d", d=HD)

        @block.sync
        def _(sp):
            sp.dma_start(wo[:, :], a["wo"]).then_inc(w_in, 16)
            sp.dma_start(wf1[:, :], a["wf1"]).then_inc(w_in, 16)
            sp.dma_start(wf2[:, :, :], a["wf2"].rearrange("(c p) n -> p c n", p=P)).then_inc(w_in, 16)
            sp.dma_start(bf1[:, :], a["bf1_t"]).then_inc(w_in, 16)
            sp.dma_start(vecs[:, :, :], a["vecs"].unsqueeze(0).broadcast_to([P, 6, C])).then_inc(w_in, 16)

            def step(c):
                if not first_round(c):
                    hold(sp, acc_ok, c, passed)
                sp.dma_start(chain[:, :, :], rows(g.chains1, c)).then_inc(ins_in[0], 16)
                sp.dma_start(values[:, :, :], rows(g.qv, c)[:, :, C:2 * C]).then_inc(ins_in[1], 16)
                if not first_round(c):
                    hold(sp, res_ok, c, passed)
                sp.dma_start(x1[:, :, :], rows(g.x1, c)).then_inc(ins_in[2], 16)
                hold(sp, res_ok, c + 1, passed)
                sp.dma_start(rows(out, c), res[:, :, :]).then_inc(stored, 16)
            chunks(sp, step)
            sp.wait_ge(stored, 16 * NCH)

        @block.gpsimd
        def _(gp):
            link = Steps(gp, pool, 4, passed)
            gp.memset(half[:, :], -0.5)

            def step(c):
                link.round(c)
                if not first_round(c):
                    hold(gp, acc_ok, c, passed)
                link(gp.tensor_copy(idx[:, :], g.sum_idx[:, bass.ds(c * CH, CH)]))
                for k in range(CH):
                    gp.indirect_dma_start(own[:, k, :], None, g.sums1,
                                          bass.IndirectOffsetOnAxis(ap=idx[:, k:k + 1], axis=0)
                                          ).then_inc(own_ok, 16)
                for norm in norms:
                    norm.root(gp, link, half, c + 1)
            chunks(gp, step)

        @block.vector
        def _(v):
            link = Steps(v, dve, 43)

            def step(c):
                link.round(c)
                v.wait_ge(own_ok, 16 * CH * (c + 1))
                v.wait_ge(ins_in[0], 16 * (c + 1))
                self_s = g.self_score[:, bass.ds(c * CH, CH), :]
                own_m, chain_m = own[:, :, C + HEADS:W1], chain[:, :, C + HEADS:W1]
                link(v.tensor_tensor(top[:, :, :], own_m, chain_m, ALU.max))
                link(v.tensor_tensor(top[:, :, :], top[:, :, :], self_s, ALU.max))
                if not first_round(c):
                    v.wait_ge(part_ok, c)
                v.tensor_tensor(part[:, 0, :, :], own_m, top[:, :, :], ALU.subtract)
                v.tensor_tensor(part[:, 1, :, :], chain_m, top[:, :, :], ALU.subtract)
                link(v.tensor_tensor(part[:, 2, :, :], self_s, top[:, :, :], ALU.subtract))
                v.nop().then_inc(diff_ok, 1)
                v.wait_ge(part_ok, c + 1)
                v.wait_ge(ins_in[1], 16 * (c + 1))
                v.tensor_tensor(den[:, 0, :, :], own[:, :, C:C + HEADS], part[:, 0, :, :], ALU.mult)
                link(v.tensor_tensor(den[:, 1, :, :], chain[:, :, C:C + HEADS], part[:, 1, :, :], ALU.mult))
                v.tensor_tensor(by_head(own[:, :, 0:C]), by_head(own[:, :, 0:C]), wide(part[:, 0, :, :]), ALU.mult)
                v.tensor_tensor(by_head(chain[:, :, 0:C]), by_head(chain[:, :, 0:C]), wide(part[:, 1, :, :]), ALU.mult)
                v.tensor_tensor(by_head(values[:, :, :]), by_head(values[:, :, :]), wide(part[:, 2, :, :]), ALU.mult)
                link(v.tensor_tensor(den[:, 0, :, :], den[:, 0, :, :], den[:, 1, :, :], ALU.add))
                link(v.scalar_tensor_tensor(den[:, 0, :, :], den[:, 0, :, :], 1e-8, part[:, 2, :, :], ALU.add, ALU.add))
                link(v.reciprocal(den[:, 0, :, :], den[:, 0, :, :]))
                link(v.tensor_tensor(acc[:, :, :], own[:, :, 0:C], chain[:, :, 0:C], ALU.add))
                link(v.tensor_tensor(acc[:, :, :], acc[:, :, :], values[:, :, :], ALU.add))
                link(v.tensor_tensor(by_head(acc[:, :, :]), by_head(acc[:, :, :]), wide(den[:, 0, :, :]), ALU.mult))
                v.nop().then_inc(acc_ok, 1)
                v.wait_ge(ins_in[2], 16 * (c + 1))
                v.wait_ge(w_in, 80)
                v.wait_ge(o_ok, 2 * c + 1)
                link(v.tensor_tensor(pre[:, :, :], x1[:, :, :], vec(0), ALU.add))
                link(v.tensor_tensor(pre[:, :, :], ps_o[:, 0:CH, :], pre[:, :, :], ALU.add))
                norms[0].stats(v, link, pre, c)
                norms[0].apply(v, link, y1, pre, c + 1)
                link(v.tensor_tensor(y1[:, :, :], y1[:, :, :], vec(2), ALU.mult))
                link(v.tensor_tensor(y1[:, :, :], y1[:, :, :], vec(3), ALU.add))
                v.nop().then_inc(y1_ok, 1)
                v.wait_ge(o_ok, 2 * c + 2)
                link(v.tensor_tensor(pre[:, :, :], y1[:, :, :], vec(1), ALU.add))
                link(v.tensor_tensor(pre[:, :, :], ps_o[:, 0:CH, :], pre[:, :, :], ALU.add))
                norms[1].stats(v, link, pre, c)
                if not first_round(c):
                    v.wait_ge(stored, 16 * c)
                norms[1].apply(v, link, res, pre, c + 1)
                link(v.tensor_tensor(res[:, :, :], res[:, :, :], vec(4), ALU.mult))
                link(v.tensor_tensor(res[:, :, :], res[:, :, :], vec(5), ALU.add))
                link(v.tensor_tensor(pre[:, :, :], res[:, :, :], x1[:, :, :], ALU.add))
                norms[2].stats(v, link, pre, c)
                norms[2].apply(v, link, res, pre, c + 1)
                v.nop().then_inc(res_ok, 1)
            chunks(v, step)

        @block.scalar
        def _(act):
            def step(c):
                act.wait_ge(diff_ok, c + 1)
                nc.scalar.activation(part[:, :, :, :], part[:, :, :, :], ACT.Exp).then_inc(part_ok, 1)
                for n in range(4):
                    lo, hi = ONE[n % 2]
                    dst = acc_t[:, lo:hi, :] if n < 2 else y1_t[:, lo * P:hi * P].rearrange("p (k n) -> p k n", n=P)
                    act.wait_ge(t_ok, 4 * c + n + 1)
                    nc.scalar.activation(dst, ps_t[n % 2][:, 0:hi - lo, :], ACT.Copy).then_inc(t_ev, 1)
                act.wait_ge(w_in, 80)
                for n in range(2 * FF // P):
                    act.wait_ge(h_ok, 8 * c + n + 1)
                    nc.scalar.activation(hid[:, n // 2, HH * (n % 2):HH * (n % 2) + HH], ps_f[n % 4][:, 0:HH],
                                         ACT.Gelu, bias=bf1[:, n // 2:n // 2 + 1]).then_inc(h_ev, 1)
            chunks(act, step)

        @block.tensor
        def _(pe):
            pe.wait_ge(w_in, 80)

            def step(c):
                for r, (ready, src) in enumerate(((acc_ok, acc), (y1_ok, y1))):
                    pe.wait_ge(ready, c + 1)
                    for n, (lo, hi) in enumerate(ONE):
                        if not (first_round(c) and r == 0):
                            pe.wait_ge(t_ev, 4 * c + 2 * r + n - 1)
                        for k in range(lo, hi):
                            last = nc.tensor.transpose(ps_t[n][:, k - lo, :], src[:, k, :], g.ident[:, :])
                        last.then_inc(t_ok, 1)
                    pe.wait_ge(t_ev, 4 * c + 2 * r + 2)
                    if r == 0:
                        for k in range(CH):
                            last = nc.tensor.matmul(ps_o[:, k, :], acc_t[:, k, :], wo[:, :], start=True, stop=True)
                        last.then_inc(o_ok, 1)
                        continue
                    for n in range(2 * FF // P):
                        if not (first_round(c) and n < 4):
                            pe.wait_ge(h_ev, 8 * c + n - 3)
                        nc.tensor.matmul(ps_f[n % 4][:, 0:HH], wf1[:, P * (n // 2):P * (n // 2) + P],
                                         y1_t[:, HH * (n % 2):HH * (n % 2) + HH], start=True,
                                         stop=True).then_inc(h_ok, 1)
                    pe.wait_ge(h_ev, 8 * c + 8)
                    for k in range(CH):
                        for m in range(FF // P):
                            last = nc.tensor.matmul(ps_o[:, k, :], hid[:, m, k * P:(k + 1) * P], wf2[:, m, :],
                                                    start=(m == 0), stop=(m == FF // P - 1))
                    last.then_inc(o_ok, 1)
            chunks(pe, step)


def program(nc, a, out):
    g = Shared()

    def dram(name, shape, dt=F32):
        return nc.dram_tensor("table_" + name, shape, dt, kind="Internal").ap()

    g.aux = dram("aux", [T, AUX], I32)
    g.resets = dram("resets", [T, HEADS, 2, P])
    g.keep = dram("keep", [T])
    g.x1 = dram("x1", [NP, C])
    g.f0 = dram("f0", [NP, C])
    g.qv = dram("qv", [NP, 2 * C])
    g.k_runs = dram("k_runs", [NP + P, C])
    g.sums0 = dram("sums0", [EP + P, W0])
    g.sums1 = dram("sums1", [EP + P, W1])
    g.chains0 = dram("chains0", [NP + T, W0])
    g.chains1 = dram("chains1", [NP + T, W1])
    with ExitStack() as ctx:
        sb, _, _ = scope(nc, ctx)
        g.rel = sb("rel", [P, T])
        g.y = sb("y", [P, T, 4])
        g.column = sb("column", [P, P])
        g.ident = sb("ident", [P, P])
        g.k_idx = sb("k_idx", [P, NB], I32)
        g.sum_idx = sb("sum_idx", [P, NB], I32)
        g.chain_idx = sb("chain_idx", [TP, TC], I32)
        g.b_scale = sb("b_scale", [P, NB])
        g.w_node = sb("w_node", [P, C])
        g.w_hidden = sb("w_hidden", [P, C])
        g.w_mix = sb("w_mix", [P, 2, C])
        g.w_after_in = sb("w_after_in", [P, 2, MUL])
        g.w_after = sb("w_after", [P, 2, C])
        g.rank0 = sb("rank0", [1, T], I32)
        g.self_score = sb("self_score", [P, NB, HEADS])
        g.w_qvk = sb("w_qvk", [P, 3 * C])
        prepare(nc, g, a)
        edge_convolution(nc, g, a)
        chain_sums(nc, g, g.sums0, g.chains0, W0, "cc_", False)
        finish_convolution(nc, g, a)
        edge_attention(nc, g, a)
        chain_sums(nc, g, g.sums1, g.chains1, W1, "ec_", True)
        finish_attention(nc, g, a, out)


def layout(inputs):
    import numpy as np

    x = np.asarray(inputs["x"])
    pad_nodes = lambda v: np.concatenate([v, np.zeros((NP - N_NODES,) + v.shape[1:], v.dtype)])
    pad_edges = lambda v, fill: np.concatenate([v, np.full((EP - N_EDGES,) + v.shape[1:], fill, v.dtype)])
    by_block = lambda v: np.ascontiguousarray(pad_nodes(np.asarray(v))[:, 0].reshape(NB, P).T)
    dst = pad_edges(np.asarray(inputs["dst"]), NP - 1)
    flat = np.concatenate([np.full(LEAD, -1, np.int32), dst, np.full(LEAD, -2, np.int32)]).astype(np.int32)
    by_tile = lambda v: np.ascontiguousarray(v.reshape(T, P).T)
    at = lambda off: flat[LEAD + off:LEAD + off + EP:P].reshape(TP, TC)
    e8 = pad_edges(np.asarray(inputs["edge_attr_8"]), 0)
    e8 = e8.reshape(NH, 4, 2, 2, P, 8).transpose(0, 1, 3, 5, 2, 4).reshape(NH, 4, 16, 2 * P)
    e8 = np.concatenate([e8, np.zeros_like(e8)], axis=2).reshape(NH, P, 2 * P)
    w = lambda k: np.asarray(inputs[k])
    return {
        "x_rows": pad_nodes(x), "x_t": pad_nodes(x).T,
        "dst_flat": flat, "dst_t": by_tile(dst), "prev_t": by_tile(flat[LEAD - 1:LEAD - 1 + EP]),
        "around": np.stack([at(-P), at(-P - 1), at(P)], axis=1),
        "src_t": pad_edges(w("src"), 0).reshape(NH, HALF, P).transpose(0, 2, 1),
        "edge4": pad_edges(w("edge_attr_4"), 0).reshape(T, P, 4).transpose(1, 0, 2),
        "edge8_t": e8, "a_in": by_block(w("node_vec1")), "b_in": by_block(w("node_vec1_n2")),
        "w1_s": w("L0_gnn_w1_s"), "w1_v": w("L0_gnn_w1_v"), "wfc1": w("L0_gnn_Wfc1"), "wfc2": w("L0_gnn_Wfc2"),
        "w2_s": w("L0_gnn_w2_s"), "w2_v": w("L0_gnn_w2_v"),
        "wq": w("L1_gnn_Wq"), "wk": w("L1_gnn_Wk"), "wv": w("L1_gnn_Wv"), "wo": w("L1_gnn_Wo"),
        "wf1": w("L1_gnn_Wf1"), "wf2": w("L1_gnn_Wf2"), "bf1_t": w("L1_gnn_bf1").reshape(FF // P, P).T,
        "vecs": np.stack([w("L1_gnn_" + k) for k in ("bo", "bf2", "g1", "b1", "g2", "b2")]),
    }


def kernel(**inputs):
    import numpy as np
    import concourse.bacc as bacc
    from concourse.bass_utils import run_bass_kernel_spmd

    nc = bacc.Bacc("TRN2", target_bir_lowering=False, num_devices=1)
    arrays = {}
    drams = {}
    for name, v in layout(inputs).items():
        v = np.ascontiguousarray(v)
        arrays["in_" + name] = v
        drams[name] = nc.dram_tensor("in_" + name, v.shape, mybir.dt.from_np(v.dtype),
                                     kind="ExternalInput").ap()
    out = nc.dram_tensor("out_0", [NP, C], F32, kind="ExternalOutput").ap()
    program(nc, drams, out)
    r = run_bass_kernel_spmd(nc, [arrays], core_ids=[0])
    return r.results[0]["out_0"][0:N_NODES]
```

```python
from contextlib import ExitStack

import concourse.bass as bass
from concourse import mybir

F32 = mybir.dt.float32
I32 = mybir.dt.int32
ALU = mybir.AluOpType
ACT = mybir.ActivationFunctionType
AX = mybir.AxisListType

P = 128
N_NODES, N_EDGES, C = 12500, 200000, 128
NB = -(-N_NODES // P)
NP = NB * P
HALF = 16
T = -(-N_EDGES // (P * HALF)) * HALF
assert T // (4 * 8) * 2 == NB
EP = T * P
NH = T // HALF
TP, TC = 112, T // 112
LEAD = 2 * P
MUL, HID, HEADS, HD, FF = 32, 64, 8, 16, 512
W0 = 8 * MUL
W1 = C + 2 * HEADS
AUX = P + 1
CH = 7
NCH = NB // CH
BIG = 1.0e30
EPS = 1e-5
INV1 = 1.0 / MUL ** 0.5
INV2 = 1.0 / (2.0 * MUL) ** 0.5
INV_SQRT3 = 1.0 / 3.0 ** 0.5
CONV_SCALE = INV2 / 16.0 ** 0.5 / HID ** 0.5


class Shared:
    pass


class Chain:

    def __init__(self, eng, sem):
        self.eng, self.sem, self.n = eng, sem, 0

    def __call__(self, ins):
        self.n += 1
        ins.then_inc(self.sem, 1)
        self.eng.wait_ge(self.sem, self.n)


def hold(eng, sem, value, passed):
    eng.wait_ge(sem, value)
    eng.sem_inc(passed, 1)


def scope(nc, ctx):
    made = []
    def sb(name, shape, dt=F32):
        return ctx.enter_context(nc.sbuf_tensor(name, shape, dt))

    def pb(name, shape, dt=F32):
        return ctx.enter_context(nc.psum_tensor(name, shape, dt))

    def sem(name):
        made.append(nc.alloc_semaphore(name))
        return made[-1]

    def clear():
        nc.all_engine_barrier()
        nc.clear_and_free_semaphores(made)
        nc.all_engine_barrier()

    ctx.callback(clear)
    return sb, pb, sem


def prepare(nc, g, a):
    with ExitStack() as ctx:
        sb, pb, sem = scope(nc, ctx)
        dst_t = sb("dst_t", [P, T], I32)
        prev_t = sb("prev_t", [P, T], I32)
        start_t = sb("start_t", [P, T])
        dst_b = sb("dst_b", [TP, TC, P], I32)
        prev_b = sb("prev_b", [TP, TC, P], I32)
        next_b = sb("next_b", [TP, TC, P], I32)
        around = sb("around", [TP, 3, TC], I32)
        first = sb("first", [TP, TC])
        first_hi = sb("first_hi", [TP, TC], I32)
        first_lo = sb("first_lo", [TP, TC], I32)
        first_hif = sb("first_hif", [TP, TC])
        first_lof = sb("first_lof", [TP, TC])
        cont = sb("cont", [TP, 5, TC])
        keep = sb("keep", [TP, TC])
        tile_no = sb("tile_no", [TP, TC])
        chain_idx = g.chain_idx
        lo_lt = sb("lo_lt", [TP, TC, P])
        hi_eq = sb("hi_eq", [TP, TC, NB])
        hi_lt = sb("hi_lt", [TP, TC, NB])
        tri = sb("tri", [P, P])
        tri_s = sb("tri_s", [P, P])
        up1 = sb("up1", [P, P])
        wrap1 = sb("wrap1", [P, P])
        ones = sb("ones", [P, P])
        ones_row = sb("ones_row", [1, T])
        totals = sb("totals", [1, T])
        incl = sb("incl", [1, T])
        last_tile = sb("last_tile", [P, NB])
        last_idx = sb("last_idx", [P, NB], I32)
        gidx = sb("gidx", [P, 2, TC], I32)
        aux = sb("aux", [P, 2, TC * AUX], I32)
        less = sb("less", [P, TC, P])
        node = sb("node", [P, NB], I32)
        nodef = sb("nodef", [P, NB])
        before = sb("before", [P, NB])
        rank_of = sb("rank_of", [P, NB])
        edge0 = sb("edge0", [P, NB + 1])
        edge1 = sb("edge1", [P, NB])
        some = sb("some", [P, NB])
        cum = sb("cum", [P, NB])
        cum_x = sb("cum_x", [P, NB])
        run = sb("run", [P, NB])
        tmp = sb("tmp", [P, 4, NB])
        xt = sb("xt", [P, 2, CH * P])
        f0 = sb("f0", [P, 2, CH, C])
        a_s = sb("a_s", [P, NB])
        ps = pb("ps_prep", [P, 8, 512])

        dst_in = sem("p_dst_in")
        loaded = sem("p_loaded")
        weights = sem("p_weights")
        xt_in = [sem(f"p_xt{i}") for i in range(2)]
        f0_out = [sem(f"p_f0{i}") for i in range(2)]
        consts = sem("p_consts")
        dve = sem("p_dve")
        pool = sem("p_pool")
        start_ok = sem("p_start")
        ranked = sem("p_ranked")
        rel_ok = sem("p_rel")
        totals_ok = sem("p_totals")
        rank0_ok = sem("p_rank0")
        aux_out = sem("p_auxout")
        keep_ok = sem("p_keep")
        hist_in = sem("p_histin")
        hist_ok = sem("p_hist")
        idx_ok = sem("p_idx")
        aux_in = [sem(f"p_aux{i}") for i in range(2)]
        aux_used = sem("p_auxused")
        edge0_ok = sem("p_edge0")
        edge1_ok = sem("p_edge1")
        cum_ok = sem("p_cum")
        run_ok = sem("p_run")
        fill_ok = sem("p_fill")
        w_ok = sem("p_w")
        a_ok = sem("p_a")
        f0_mm = sem("p_f0mm")
        f0_ev = sem("p_f0ev")
        stored = sem("p_stored")
        y_in = sem("p_y")
        stores = [0]
        block = ctx.enter_context(nc.Block())

        flat = lambda off: a["dst_flat"][LEAD + off:LEAD + off + EP].rearrange("(p c e) -> p c e", c=TC, e=P)
        f0_v = g.f0.rearrange("(h p) w -> p h w", p=P)

        @block.sync
        def _(sp):
            def store(dst, src, **how):
                sp.dma_start(dst, src, **how).then_inc(stored, 16)
                stores[0] += 16

            sp.dma_start(dst_t[:, :], a["dst_t"]).then_inc(dst_in, 16)
            sp.dma_start(prev_t[:, :], a["prev_t"]).then_inc(dst_in, 16)
            sp.dma_start(dst_b[:, :, :], flat(0)).then_inc(dst_in, 16)
            sp.dma_start(prev_b[:, :, :], flat(-1)).then_inc(loaded, 16)
            sp.dma_start(next_b[:, :, :], flat(1)).then_inc(loaded, 16)
            sp.dma_start(around[:, :, :], a["around"]).then_inc(loaded, 16)
            sp.wait_ge(w_ok, 1)
            sp.dma_start(g.w_node[0:MUL, 0:MUL], a["w1_s"]).then_inc(weights, 16)
            for i in range(3):
                sp.dma_start(g.w_node[MUL + i:P:3, MUL * (1 + i):MUL * (2 + i)], a["w1_v"]).then_inc(weights, 16)
            for q in range(4):
                for h in range(2):
                    sp.dma_start(g.w_hidden[32 * q + 8 * h:32 * q + 8 * h + 8, HID * h:HID * h + HID],
                                 a["wfc1"]).then_inc(weights, 16)
            for h in range(2):
                sp.dma_start(g.w_mix[HID * h:HID * h + HID, h, :], a["wfc2"]).then_inc(weights, 16)
            for m, rows in enumerate(((a["w2_s"][0], a["w2_s"][1], a["w2_v"][0], a["w2_v"][0]),
                                      (a["w2_v"][0], a["w2_v"][1], a["w2_v"][1], a["w2_v"][1]))):
                for q, src in enumerate(rows):
                    sp.dma_start(g.w_after_in[32 * q:32 * q + 32, m, :], src).then_inc(weights, 16)
            sp.dma_start(g.w_qvk[:, 0:C], a["wq"]).then_inc(weights, 16)
            sp.dma_start(g.w_qvk[:, C:2 * C], a["wv"]).then_inc(weights, 16)
            sp.dma_start(g.w_qvk[:, 2 * C:3 * C], a["wk"]).then_inc(weights, 16)
            sp.dma_start(a_s[:, :], a["a_in"]).then_inc(weights, 16)
            sp.dma_start(g.b_scale[:, :], a["b_in"]).then_inc(weights, 16)
            def load_xt(c):
                sp.dma_start(xt[:, c % 2, :], a["x_t"][:, c * CH * P:(c + 1) * CH * P]).then_inc(xt_in[c % 2], 16)

            load_xt(0)
            load_xt(1)
            sp.wait_ge(dst_in, 48)
            store(g.aux[:, 0:P].rearrange("(p c) e -> p c e", c=TC), dst_b[:, :, :])
            sp.wait_ge(rank0_ok, 1)
            store(g.aux[:, P:P + 1], g.rank0[0:1, :], allow_slow_non_contiguous=True)
            sp.wait_ge(stored, stores[0])
            sp.nop().then_inc(aux_out, 1)
            sp.wait_ge(keep_ok, 1)
            store(g.keep.rearrange("(p c) -> p c", c=TC), keep[:, :])
            sp.wait_ge(fill_ok, 1)
            store(g.sums0[EP:EP + P, :], g.none0[:, :])
            store(g.sums1[EP:EP + P, :], g.none1[:, :])
            store(g.k_runs[NP:NP + P, :], g.none0[:, 0:C])
            for c in range(NCH):
                sp.wait_ge(f0_ev, (c + 1) * CH)
                sp.dma_start(f0_v[:, CH * c:CH * c + CH, :], f0[:, c % 2, :, :]).then_inc(f0_out[c % 2], 16)
                if c + 2 < NCH:
                    load_xt(c + 2)
            sp.dma_start(g.y[:, :, :], a["edge4"]).then_inc(y_in, 16)
            sp.wait_ge(stored, stores[0])
            sp.wait_ge(y_in, 16)
            for i in range(2):
                sp.wait_ge(f0_out[i], 16 * NCH // 2)

        @block.gpsimd
        def _(gp):
            link = Chain(gp, pool)
            gp.memset(ones[:, :], 1.0)
            gp.memset(ones_row[:, :], 1.0)
            gp.memset(g.none0[:, :], 0.0)
            gp.memset(g.none1[:, 0:C + HEADS], 0.0)
            gp.memset(g.none1[:, C + HEADS:W1], -BIG)
            link(gp.memset(g.ident[:, :], 0.0))
            gp.nop().then_inc(fill_ok, 1)
            gp.affine_select(out=g.ident[:, :], in_=g.ident[:, :], compare_op=ALU.not_equal, fill=1.0, base=0,
                             pattern=[[-1, P]], channel_multiplier=1)
            gp.iota(g.column[:, :], pattern=[[1, P]], base=0, channel_multiplier=0,
                    allow_small_or_imprecise_dtypes=True)
            gp.iota(node[:, :], pattern=[[P, NB]], base=0, channel_multiplier=1)
            gp.iota(nodef[:, :], pattern=[[P, NB]], base=0, channel_multiplier=1,
                    allow_small_or_imprecise_dtypes=True)
            gp.iota(tile_no[:, :], pattern=[[1, TC]], base=NP, channel_multiplier=TC,
                    allow_small_or_imprecise_dtypes=True)
            link(gp.affine_select(out=tri[:, :], in_=ones[:, :], compare_op=ALU.is_ge, fill=0.0, base=0,
                                  pattern=[[1, P]], channel_multiplier=-1))
            link(gp.affine_select(out=tri[:, :], in_=tri[:, :], compare_op=ALU.is_ge, fill=0.0, base=-1,
                                  pattern=[[0, P]], channel_multiplier=1))
            link(gp.affine_select(out=tri_s[:, :], in_=ones[:, :], compare_op=ALU.is_ge, fill=0.0, base=-1,
                                  pattern=[[1, P]], channel_multiplier=-1))
            link(gp.memset(up1[:, :], 0.0))
            link(gp.memset(wrap1[:, :], 0.0))
            link(gp.affine_select(out=up1[:, :], in_=up1[:, :], compare_op=ALU.not_equal, fill=1.0, base=-1,
                                  pattern=[[-1, P]], channel_multiplier=1))
            link(gp.affine_select(out=wrap1[:, :], in_=wrap1[:, :], compare_op=ALU.not_equal, fill=1.0, base=P - 1,
                                  pattern=[[-1, P]], channel_multiplier=P))
            gp.nop().then_inc(consts, 1)
            gp.wait_ge(idx_ok, 1)
            gp.wait_ge(aux_out, 1)
            for r in range(NCH // 2):
                if r >= 2:
                    gp.wait_ge(aux_used, r - 1)
                for k in range(TC):
                    gp.indirect_dma_start(aux[:, r % 2, k * AUX:(k + 1) * AUX], None, g.aux,
                                          bass.IndirectOffsetOnAxis(ap=last_idx[:, TC * r + k:TC * r + k + 1], axis=0)
                                          ).then_inc(aux_in[r % 2], 16)

        @block.vector
        def _(v):
            link = Chain(v, dve)
            v.memset(g.w_node[:, :], 0.0)
            v.memset(g.w_mix[:, :, :], 0.0)
            v.memset(g.w_hidden[:, :], 0.0).then_inc(w_ok, 1)
            link(v.memset(g.w_after[:, :, :], 0.0))
            v.wait_ge(dst_in, 48)
            v.wait_ge(consts, 1)
            v.tensor_tensor(start_t[:, :], dst_t[:, :], prev_t[:, :], ALU.not_equal).then_inc(start_ok, 1)
            link(v.tensor_single_scalar(first_hi[:, :], dst_b[:, :, 0], 7, ALU.logical_shift_right))
            link(v.tensor_single_scalar(first_lo[:, :], dst_b[:, :, 0], P - 1, ALU.bitwise_and))
            v.tensor_copy(first_hif[:, :], first_hi[:, :])
            v.tensor_copy(first[:, :], dst_b[:, :, 0])
            link(v.tensor_copy(first_lof[:, :], first_lo[:, :]))
            for c in range(TC):
                v.tensor_scalar(lo_lt[:, c, :], g.column[0:TP, :], first_lof[:, c:c + 1], None, ALU.is_gt)
                v.tensor_scalar(hi_eq[:, c, :], g.column[0:TP, 0:NB], first_hif[:, c:c + 1], None, ALU.is_equal)
                v.tensor_scalar(hi_lt[:, c, :], g.column[0:TP, 0:NB], first_hif[:, c:c + 1], None,
                                ALU.is_gt).then_inc(hist_in, 1)
            for k in range(4):
                v.wait_ge(ranked, k + 1)
                v.tensor_copy(g.rel[:, k * 392:(k + 1) * 392], ps[:, k, 0:392]).then_inc(rel_ok, 1)
            for k in range(4):
                v.wait_ge(totals_ok, k + 1)
                link(v.tensor_copy(totals[0:1, k * 392:(k + 1) * 392], ps[0:1, 4 + k, 0:392]))
            link(v.tensor_tensor_scan(incl[:, :], ones_row[:, :], totals[:, :], 0.0, ALU.mult, ALU.add))
            link(v.tensor_tensor(incl[:, :], incl[:, :], totals[:, :], ALU.subtract))
            v.scalar_tensor_tensor(g.rank0[:, :], incl[:, :], -1.0, start_t[0:1, :], ALU.add,
                                   ALU.add).then_inc(rank0_ok, 1)
            v.wait_ge(weights, 16 * 27)
            comp = lambda i: g.w_after[:, :, MUL:C].rearrange("p m (w i) -> p m i w", i=3)[:, :, i, :]
            v.tensor_copy(g.w_after[0:32, 0, 0:MUL], g.w_after_in[0:32, 0, :])
            v.tensor_scalar(g.w_after[32:64, 0, 0:MUL], g.w_after_in[32:64, 0, :], INV_SQRT3, None, ALU.mult)
            for m, q, i in ((0, 2, 0), (0, 3, 1), (1, 0, 2), (1, 1, 0), (1, 2, 1), (1, 3, 2)):
                v.tensor_copy(comp(i)[32 * q:32 * q + 32, m, :], g.w_after_in[32 * q:32 * q + 32, m, :])
            v.tensor_scalar(g.b_scale[:, :], g.b_scale[:, :], CONV_SCALE, None, ALU.mult)
            v.tensor_scalar(a_s[:, :], a_s[:, :], INV1, None, ALU.mult).then_inc(a_ok, 1)
            v.wait_ge(loaded, 48)
            for m, other in enumerate((prev_b, next_b)):
                out = g.reset[:, :, m, :]
                link(v.tensor_tensor(out, dst_b[:, :, :], other[:, :, :], ALU.not_equal))
                link(v.tensor_scalar(out, out, -BIG, None, ALU.mult))
            v.memset(g.reset[:, :, 1, P - 1:P], -BIG)
            v.tensor_tensor(cont[:, 0, :], dst_b[:, :, 0], prev_b[:, :, 0], ALU.is_equal)
            v.tensor_tensor(cont[:, 1, :], around[:, 0, :], around[:, 1, :], ALU.is_equal)
            v.tensor_tensor(cont[:, 2, :], around[:, 0, :], dst_b[:, :, 0], ALU.is_equal)
            v.tensor_tensor(cont[:, 3, :], around[:, 2, :], dst_b[:, :, P - 1], ALU.is_equal)
            link(v.tensor_tensor(cont[:, 4, :], around[:, 2, :], dst_b[:, :, 0], ALU.is_equal))
            link(v.tensor_tensor(cont[:, 1, :], cont[:, 1, :], cont[:, 2, :], ALU.mult))
            v.tensor_tensor(keep[:, :], cont[:, 1, :], cont[:, 0, :], ALU.mult).then_inc(keep_ok, 1)
            link(v.tensor_tensor(cont[:, 3, :], cont[:, 3, :], cont[:, 4, :], ALU.mult))
            link(v.tensor_tensor(cont[:, 3, :], cont[:, 0, :], cont[:, 3, :], ALU.is_gt))
            link(v.tensor_tensor(cont[:, 0, :], first[:, :], tile_no[:, :], ALU.subtract))
            link(v.tensor_tensor(cont[:, 0, :], cont[:, 0, :], cont[:, 3, :], ALU.mult))
            link(v.tensor_tensor(chain_idx[:, :], cont[:, 0, :], tile_no[:, :], ALU.add))
            v.wait_ge(hist_ok, 1)
            link(v.tensor_scalar(last_tile[:, :], ps[:, 0, 0:NB], -1.0, 0.0, ALU.add, ALU.max))
            v.tensor_copy(last_idx[:, :], last_tile[:, :]).then_inc(idx_ok, 1)
            for r in range(NCH // 2):
                v.wait_ge(aux_in[r % 2], 16 * TC * (r // 2 + 1))
                rows = aux[:, r % 2, :].rearrange("p (k w) -> p k w", w=AUX)
                cols = slice(TC * r, TC * r + TC)
                link(v.tensor_tensor(less[:, :, :], rows[:, :, 0:P],
                                     node[:, cols].unsqueeze(2).broadcast_to([P, TC, P]), ALU.is_lt))
                link(v.tensor_reduce(before[:, cols], less[:, :, :], AX.X, ALU.add))
                v.tensor_copy(rank_of[:, cols], rows[:, :, P]).then_inc(aux_used, 1)
            v.memset(edge0[:, NB:NB + 1], float(EP))
            link(v.memset(cum_x[:, 0:1], 0.0))
            v.scalar_tensor_tensor(edge0[:, 0:NB], last_tile[:, :], float(P), before[:, :], ALU.mult,
                                   ALU.add).then_inc(edge0_ok, 1)
            v.wait_ge(edge0_ok, 1)
            v.wait_ge(edge1_ok, 1)
            link(v.tensor_tensor(some[:, :], ps[:, 1, 0:NB], edge0[:, 0:NB], ALU.is_gt))
            link(v.tensor_tensor_scan(cum[:, :], ones[:, 0:NB], some[:, :], 0.0, ALU.mult, ALU.add))
            v.tensor_copy(cum_x[:, 1:NB], cum[:, 0:NB - 1]).then_inc(cum_ok, 1)
            v.wait_ge(run_ok, 1)
            link(v.tensor_copy(run[:, :], ps[:, 2, 0:NB]))
            link(v.tensor_tensor(tmp[:, 0, :], nodef[:, :], run[:, :], ALU.subtract))
            link(v.tensor_scalar(tmp[:, 0, :], tmp[:, 0, :], ps[:, 3, 0:1], None, ALU.add))
            link(v.tensor_tensor(tmp[:, 1, :], run[:, :], tmp[:, 0, :], ALU.subtract))
            link(v.tensor_tensor(tmp[:, 1, :], tmp[:, 1, :], some[:, :], ALU.mult))
            link(v.tensor_tensor(g.k_idx[:, :], tmp[:, 1, :], tmp[:, 0, :], ALU.add))
            link(v.tensor_scalar(tmp[:, 0, :], before[:, :], float(P), None, ALU.is_equal))
            link(v.tensor_tensor(tmp[:, 1, :], run[:, :], rank_of[:, :], ALU.subtract))
            link(v.tensor_tensor(tmp[:, 2, :], tmp[:, 1, :], tmp[:, 0, :], ALU.mult))
            link(v.tensor_tensor(tmp[:, 1, :], tmp[:, 1, :], tmp[:, 2, :], ALU.subtract))
            link(v.tensor_tensor(tmp[:, 0, :], last_tile[:, :], tmp[:, 0, :], ALU.add))
            link(v.scalar_tensor_tensor(tmp[:, 0, :], tmp[:, 0, :], float(P), tmp[:, 1, :], ALU.mult, ALU.add))
            link(v.scalar_tensor_tensor(tmp[:, 0, :], tmp[:, 0, :], -float(EP), some[:, :], ALU.add, ALU.mult))
            link(v.tensor_scalar(g.sum_idx[:, :], tmp[:, 0, :], float(EP), None, ALU.add))

        @block.scalar
        def _(act):
            act.wait_ge(a_ok, 1)
            for c in range(NCH):
                if c >= 2:
                    act.wait_ge(f0_out[c % 2], 16 * (c // 2))
                for k in range(CH):
                    b = CH * c + k
                    act.wait_ge(f0_mm, b + 1)
                    nc.scalar.activation(f0[:, c % 2, k, :], ps[:, 4 + b % 4, 0:C], ACT.Copy,
                                         scale=a_s[:, b:b + 1]).then_inc(f0_ev, 1)

        @block.tensor
        def _(pe):
            pe.wait_ge(consts, 1)
            pe.wait_ge(start_ok, 1)
            for k in range(4):
                nc.tensor.matmul(ps[:, k, 0:392], tri[:, :], start_t[:, k * 392:(k + 1) * 392],
                                 start=True, stop=True).then_inc(ranked, 1)
            for k in range(4):
                nc.tensor.matmul(ps[0:1, 4 + k, 0:392], ones[:, 0:1], start_t[:, k * 392:(k + 1) * 392],
                                 start=True, stop=True).then_inc(totals_ok, 1)
            pe.wait_ge(rel_ok, 4)
            for c in range(TC):
                pe.wait_ge(hist_in, c + 1)
                nc.tensor.matmul(ps[:, 0, 0:NB], lo_lt[:, c, :], hi_eq[:, c, :], start=(c == 0), stop=False)
                last = nc.tensor.matmul(ps[:, 0, 0:NB], ones[0:TP, :], hi_lt[:, c, :], start=False,
                                        stop=(c == TC - 1))
            last.then_inc(hist_ok, 1)
            pe.wait_ge(weights, 16 * 27)
            pe.wait_ge(rank0_ok, 1)
            for c in range(NCH):
                pe.wait_ge(xt_in[c % 2], 16 * (c // 2 + 1))
                for k in range(CH):
                    b = CH * c + k
                    if b >= 4:
                        pe.wait_ge(f0_ev, b - 3)
                    nc.tensor.matmul(ps[:, 4 + b % 4, 0:C], xt[:, c % 2, k * P:(k + 1) * P], g.w_node[:, :],
                                     start=True, stop=True).then_inc(f0_mm, 1)
            pe.wait_ge(edge0_ok, 1)
            nc.tensor.matmul(ps[:, 1, 0:NB], up1[:, :], edge0[:, 0:NB], start=True, stop=False)
            nc.tensor.matmul(ps[:, 1, 0:NB], wrap1[:, :], edge0[:, 1:NB + 1], start=False,
                             stop=True).then_inc(edge1_ok, 1)
            pe.wait_ge(cum_ok, 1)
            nc.tensor.matmul(ps[:, 2, 0:NB], tri_s[:, :], some[:, :], start=True, stop=False)
            nc.tensor.matmul(ps[:, 2, 0:NB], ones[:, :], cum_x[:, :], start=False, stop=True)
            nc.tensor.matmul(ps[:, 3, 0:1], ones[:, :], cum[:, NB - 1:NB], start=True,
                             stop=True).then_inc(run_ok, 1)


def edge_convolution(nc, g, a):
    with ExitStack() as ctx:
        sb, pb, sem = scope(nc, ctx)
        QT = 4
        NG = T // QT
        U = 8
        idx = sb("c_idx", [P, 2, HALF], I32)
        attr = sb("c_attr", [P, 2, 2 * P])
        x_src = sb("c_x", [P, 4, QT, C])
        hid = sb("c_hid", [P, 2, 2 * P])
        hot = sb("c_hot", [P, 2, QT, P])
        msg = sb("c_msg", [P, 2, QT, W0])
        we = sb("c_we", [P, QT, 2 * MUL])
        wy = sb("c_wy", [P, QT, MUL])
        vy = sb("c_vy", [P, QT, 3 * MUL])
        dot = sb("c_dot", [P, QT, MUL])
        out = sb("c_out", [P, 2, QT, W0])
        ps_h = [pb(f"c_ps_h{i}", [P, 512]) for i in range(2)]
        ps_w = [pb(f"c_ps_w{i}", [P, QT, P]) for i in range(2)]
        ps_s = [[pb(f"c_ps_s{i}{j}", [P, 512]) for j in range(2)] for i in range(2)]

        idx_in = [sem(f"c_idx_in{i}") for i in range(2)]
        attr_in = [sem(f"c_attr_in{i}") for i in range(2)]
        gathered = [sem(f"c_gathered{i}") for i in range(4)]
        stored = [sem(f"c_stored{i}") for i in range(2)]
        hidden = sem("c_hidden")
        silu_ok = sem("c_silu")
        mixed = sem("c_mixed")
        hot_ok = sem("c_hot_ok")
        dve = sem("c_dve")
        msg_ok = sem("c_msg_ok")
        summed = sem("c_summed")
        staged = sem("c_staged")
        cleared = sem("c_cleared")
        passed = sem("c_passed")
        block = ctx.enter_context(nc.Block())

        table = g.sums0[0:EP, :].rearrange("(t r) w -> r t w", r=P)

        def groups(eng, step):
            for u in range(U):
                step(0, u)
            with eng.Fori(1, NG // U - 1) as i:
                for u in range(U):
                    step(i, u)
            for u in range(U):
                step(NG // U - 1, u)

        def early(i, u, n):
            return isinstance(i, int) and U * i + u < n

        def late(i, u, n):
            return isinstance(i, int) and U * i + u >= NG - n

        @block.sync
        def _(sp):
            def load(i, h):
                if not (isinstance(i, int) and i == 0):
                    hold(sp, hidden, i * U + 4 * h - 4, passed)
                    for q in range(4):
                        hold(sp, gathered[q], 16 * QT * (2 * i + h - 1), passed)
                sp.dma_start(attr[:, h, :], a["edge8_t"][bass.ds(i * 2 + h, 1), :, :].rearrange("o p n -> p (o n)")
                             ).then_inc(attr_in[h], 16)
                sp.dma_start(idx[:, h, :], a["src_t"][bass.ds(i * 2 + h, 1), :, :].rearrange("o p n -> p (o n)")
                             ).then_inc(idx_in[h], 16)

            def store(i, u):
                j = i * U + u
                hold(sp, staged, j + 1, passed)
                sp.dma_start(table[:, bass.ds(j * QT, QT), :], out[:, u % 2, :, :]).then_inc(stored[u % 2], 16)

            def clear(i):
                sp.dma_start(g.chains0[bass.ds(i * 2 * P, 2 * P), :].rearrange("(h p) w -> p h w", p=P),
                             g.none0[:, :].unsqueeze(1).broadcast_to([P, 2, W0])).then_inc(cleared, 16)

            load(0, 0)
            load(0, 1)
            clear(0)
            for u in range(U):
                store(0, u)
                if u % 4 == 3:
                    load(1, u // 4)
            for begin, end in ((1, HEADS + 1), (HEADS + 1, NG // U - 1)):
                with sp.Fori(begin, end) as i:
                    clear(i)
                    if begin == 1:
                        sp.dma_start(g.resets[:, bass.ds(i - 1, 1), :, :].rearrange("(p c) o m e -> p c (o m e)", c=TC),
                                     g.reset[:, :, :, :].rearrange("p c m e -> p c (m e)")).then_inc(cleared, 16)
                    for u in range(U):
                        store(i, u)
                        if u % 4 == 3:
                            load(i + 1, u // 4)
            clear(NG // U - 1)
            for u in range(U):
                store(NG // U - 1, u)
            for b in range(2):
                sp.wait_ge(stored[b], 16 * NG // 2)
            sp.wait_ge(cleared, 16 * (NG // U + HEADS))

        @block.gpsimd
        def _(gp):
            def step(i, u):
                h = u // 4
                if u % 4 == 0:
                    hold(gp, idx_in[h], 16 * (i + 1), passed)
                if not early(i, u, 4):
                    hold(gp, msg_ok, i * U + (u - 3), passed)
                for k in range(QT):
                    c = QT * (u % 4) + k
                    gp.indirect_dma_start(x_src[:, u % 4, k, :], None, g.f0,
                                          bass.IndirectOffsetOnAxis(ap=idx[:, h, c:c + 1], axis=0)
                                          ).then_inc(gathered[u % 4], 16)
            groups(gp, step)

        @block.scalar
        def _(act):
            def silu(i, u):
                act.wait_ge(hidden, i * U + u + 1)
                if not early(i, u, 2):
                    act.wait_ge(mixed, i * U + (u - 1))
                nc.scalar.activation(hid[:, u % 2, :], ps_h[u % 2][:, 0:2 * P], ACT.Silu,
                                     scale=1.0 / HEADS ** 0.5).then_inc(silu_ok, 1)

            def stage(i, u):
                act.wait_ge(summed, i * U + u + 1)
                if not early(i, u, 2):
                    act.wait_ge(stored[u % 2], 16 * (4 * i + (u - 2) // 2 + 1))
                for m in range(2):
                    last = nc.scalar.activation(out[:, u % 2, 2 * m:2 * m + 2, :],
                                                ps_s[u % 2][m][:, :].rearrange("p (k w) -> p k w", k=2), ACT.Copy)
                last.then_inc(staged, 1)

            def step(i, u):
                if not late(i, u, 1):
                    if u + 1 < U:
                        silu(i, u + 1)
                    else:
                        silu(i + 1, 0)
                if not early(i, u, 1):
                    if u:
                        stage(i, u - 1)
                    else:
                        stage(i - 1, U - 1)

            silu(0, 0)
            groups(act, step)
            stage(NG // U - 1, U - 1)

        @block.vector
        def _(v):
            STEPS = 8

            def step(i, u):
                j = i * U + u
                b = u % 2
                w = ps_w[b][:, :, :].rearrange("p k (m c) -> p k m c", m=4)
                x = x_src[:, u % 4, :, :].rearrange("p k (m c) -> p k m c", m=4)
                y = g.y[:, bass.ds(j * QT, QT), :]
                y0 = y[:, :, 0:1].broadcast_to([P, QT, MUL])
                y3 = y[:, :, 1:4].unsqueeze(3).broadcast_to([P, QT, 3, MUL])
                o = msg[:, b, :, :]
                done = [0]

                def sig(ins):
                    ins.then_inc(dve, 1)
                    done[0] += 1
                    return done[0]

                def after(n):
                    v.wait_ge(dve, j * STEPS + n)

                if not early(i, u, 2):
                    v.wait_ge(summed, j - 1)
                for k in range(QT):
                    last = v.tensor_scalar(hot[:, b, k, :], g.column[:, :], g.rel[:, bass.ds(j * QT + k, 1)], None,
                                           ALU.is_equal)
                last.then_inc(hot_ok, 1)
                v.wait_ge(gathered[u % 4], 16 * QT * (2 * i + u // 4 + 1))
                n_vy = sig(v.tensor_tensor(vy[:, :, :].rearrange("p k (m c) -> p k m c", m=3), x[:, :, 1:4, :], y3,
                                           ALU.mult))
                v.wait_ge(mixed, j + 1)
                n_we = sig(v.tensor_tensor(we[:, :, :].rearrange("p k (m c) -> p k m c", m=2), w[:, :, 0:2, :],
                                           x[:, :, 0:1, :].broadcast_to([P, QT, 2, MUL]), ALU.mult))
                n_wy = sig(v.tensor_tensor(wy[:, :, :], w[:, :, 2, :], y0, ALU.mult))
                after(n_vy)
                n_d = sig(v.tensor_tensor(dot[:, :, :], vy[:, :, 0:MUL], vy[:, :, MUL:2 * MUL], ALU.add))
                after(n_we)
                n_m0 = sig(v.tensor_tensor(o[:, :, 0:MUL], we[:, :, 0:MUL], y0, ALU.mult))
                v.tensor_tensor(o[:, :, 2 * MUL:5 * MUL].rearrange("p k (m c) -> p k m c", m=3),
                                we[:, :, MUL:2 * MUL].unsqueeze(2).broadcast_to([P, QT, 3, MUL]), y3, ALU.mult)
                after(n_d)
                n_d2 = sig(v.tensor_tensor(dot[:, :, :], dot[:, :, :], vy[:, :, 2 * MUL:3 * MUL], ALU.add))
                after(n_wy)
                n_m2 = sig(v.tensor_tensor(o[:, :, 5 * MUL:8 * MUL].rearrange("p k (m c) -> p k m c", m=3),
                                           wy[:, :, :].unsqueeze(2).broadcast_to([P, QT, 3, MUL]), x[:, :, 1:4, :],
                                           ALU.mult))
                after(n_d2)
                n_m3 = sig(v.tensor_tensor(o[:, :, MUL:2 * MUL], w[:, :, 3, :], dot[:, :, :], ALU.mult))
                assert done[0] == STEPS
                after(n_m3)
                v.nop().then_inc(msg_ok, 1)
            groups(v, step)

        @block.tensor
        def _(pe):
            def first_layer(i, u):
                if u % 4 == 0:
                    pe.wait_ge(attr_in[u // 4], 16 * (i + 1))
                if not early(i, u, 2):
                    pe.wait_ge(silu_ok, i * U + (u - 1))
                q = 32 * (u % 4)
                nc.tensor.matmul(ps_h[u % 2][:, 0:2 * P], g.w_hidden[q:q + 16, :], attr[q:q + 16, u // 4, :],
                                 start=True, stop=True).then_inc(hidden, 1)

            def second_layer(i, u):
                pe.wait_ge(silu_ok, i * U + u + 1)
                if not early(i, u, 2):
                    pe.wait_ge(msg_ok, i * U + (u - 1))
                for pair in range(2):
                    last = nc.tensor.matmul(ps_w[u % 2][:, 2 * pair:2 * pair + 2, :],
                                            hid[:, u % 2, P * pair:P * pair + P], g.w_mix[:, :, :],
                                            start=True, stop=True)
                last.then_inc(mixed, 1)

            def sums(i, u):
                pe.wait_ge(hot_ok, i * U + u + 1)
                pe.wait_ge(msg_ok, i * U + u + 1)
                if not early(i, u, 2):
                    pe.wait_ge(staged, i * U + (u - 1))
                for k in range(QT):
                    last = nc.tensor.matmul(ps_s[u % 2][k // 2][:, W0 * (k % 2):W0 * (k % 2) + W0],
                                            hot[:, u % 2, k, :], msg[:, u % 2, k, :], start=True, stop=True)
                last.then_inc(summed, 1)

            def step(i, u):
                second_layer(i, u)
                if not late(i, u, 1):
                    if u + 1 < U:
                        first_layer(i, u + 1)
                    else:
                        first_layer(i + 1, 0)
                if not early(i, u, 1):
                    if u:
                        sums(i, u - 1)
                    else:
                        sums(i - 1, U - 1)

            first_layer(0, 0)
            groups(pe, step)
            sums(NG // U - 1, U - 1)


def chain_sums(nc, g, rows, table, width, name, heads, own):
    with ExitStack() as ctx:
        sb, pb, sem = scope(nc, ctx)
        NQ = T // 4
        row_in = sb(name + "row", [TP, TC, width])
        row_out = sb(name + "out", [TP, TC, width])
        keep = sb(name + "keep", [P, T])
        parts = [(0, C), (C, 2 * C)] if not heads else [(0, C), (C, C + HEADS), (C + HEADS, width)]
        turned = [sb(f"{name}t{i}", [b - a, T]) for i, (a, b) in enumerate(parts)]
        total = [sb(f"{name}s{i}", [b - a, T]) for i, (a, b) in enumerate(parts)]
        if heads:
            reset = sb(name + "reset", [HEADS, T + 1])
            spread = sb(name + "spread", [HEADS, C])
            weight = sb(name + "weight", [HEADS, T])
        ps = pb(name + "ps", [P, 8, 512])
        loaded = sem(name + "loaded")
        pe_ok = sem(name + "pe")
        ev_ok = sem(name + "ev")
        total_ok = sem(name + "total")
        back_ok = sem(name + "back")
        row_ok = sem(name + "rowok")
        scattered = sem(name + "scattered")
        gathered = sem(name + "gathered")
        dve = sem(name + "dve")
        weighed = sem(name + "weighed")
        diff_ok = sem(name + "diff")
        spread_ok = sem(name + "spread")
        wide_ok = sem(name + "wide")
        wide_used = sem(name + "wideused")
        block = ctx.enter_context(nc.Block())
        jobs = [(c, i) for i in reversed(range(len(parts))) for c in range(TC)]

        @block.sync
        def _(sp):
            sp.dma_start(row_in[:, :, :],
                         rows[0:EP, :].rearrange("(p c r) w -> p c r w", c=TC, r=P)[:, :, 0, :]).then_inc(loaded, 16)
            sp.dma_start(keep[:, :], g.keep.unsqueeze(0).broadcast_to([P, T])).then_inc(loaded, 16)

        @block.tensor
        def _(pe):
            pe.wait_ge(loaded, 32)
            for n, (c, i) in enumerate(jobs):
                lo, hi = parts[i]
                if n >= 4:
                    pe.wait_ge(ev_ok, n - 3)
                nc.tensor.transpose(ps[0:hi - lo, n % 4, 0:TP], row_in[:, c, lo:hi],
                                    g.ident[0:TP, 0:TP]).then_inc(pe_ok, 1)
            if heads:
                pe.wait_ge(weighed, 1)
                pe.wait_ge(spread_ok, 1)
                pe.wait_ge(ev_ok, len(jobs))
                for k in range(4):
                    nc.tensor.matmul(ps[:, k, 0:NQ], spread[:, :], weight[:, k * NQ:(k + 1) * NQ], start=True,
                                     stop=True).then_inc(wide_ok, 1)
            pe.wait_ge(total_ok, 1)
            for n, (c, i) in enumerate(jobs):
                lo, hi = parts[i]
                if n >= 4:
                    pe.wait_ge(row_ok, n - 3)
                nc.tensor.transpose(ps[0:TP, 4 + n % 4, 0:hi - lo],
                                    total[i][:, :].rearrange("w (p c) -> w c p", c=TC)[:, c, :],
                                    g.ident[0:hi - lo, 0:hi - lo]).then_inc(back_ok, 1)

        @block.scalar
        def _(act):
            for n, (c, i) in enumerate(jobs):
                lo, hi = parts[i]
                act.wait_ge(pe_ok, n + 1)
                nc.scalar.activation(turned[i][:, :].rearrange("w (p c) -> w c p", c=TC)[:, c, :],
                                     ps[0:hi - lo, n % 4, 0:TP], ACT.Copy).then_inc(ev_ok, 1)
            if heads:
                act.wait_ge(diff_ok, 1)
                nc.scalar.activation(weight[:, :], weight[:, :], ACT.Exp).then_inc(weighed, 1)
            for n, (c, i) in enumerate(jobs):
                lo, hi = parts[i]
                act.wait_ge(back_ok, n + 1)
                nc.scalar.activation(row_out[:, c, lo:hi], ps[0:TP, 4 + n % 4, 0:hi - lo],
                                     ACT.Copy).then_inc(row_ok, 1)

        @block.vector
        def _(v):
            link = Chain(v, dve)
            v.wait_ge(loaded, 32)
            v.wait_ge(ev_ok, len(jobs))
            if heads:
                acc, den, top = turned
                link(v.tensor_scalar(reset[:, 0:T], keep[0:HEADS, :], -1.0, BIG, ALU.add, ALU.mult))
                link(v.memset(reset[:, T:T + 1], -BIG))
                link(v.tensor_tensor_scan(weight[:, :], reset[:, 0:T], top[:, :], -BIG, ALU.add, ALU.max))
                link(v.tensor_tensor_scan(total[2][:, ::-1], reset[:, 1:T + 1][:, ::-1], weight[:, ::-1], -BIG,
                                          ALU.add, ALU.max))
                link(v.tensor_tensor(weight[:, :], top[:, :], total[2][:, :], ALU.subtract))
                v.nop().then_inc(diff_ok, 1)
                v.wait_ge(weighed, 1)
                link(v.tensor_tensor(den[:, :], den[:, :], weight[:, :], ALU.mult))
                for k in range(4):
                    v.wait_ge(wide_ok, k + 1)
                    link(v.tensor_tensor(acc[:, k * NQ:(k + 1) * NQ], acc[:, k * NQ:(k + 1) * NQ],
                                         ps[:, k, 0:NQ], ALU.mult))
            for i in range(2):
                link(v.tensor_tensor_scan(total[i][:, :], keep[0:turned[i].shape[0], :], turned[i][:, :], 0.0,
                                          ALU.mult, ALU.add))
            v.nop().then_inc(total_ok, 1)

        @block.gpsimd
        def _(gp):
            if heads:
                gp.memset(spread[:, :], 1.0).then_inc(wide_used, 1)
                gp.wait_ge(wide_used, 1)
                gp.affine_select(out=spread[:, :], in_=spread[:, :], compare_op=ALU.is_ge, fill=0.0, base=0,
                                 pattern=[[1, C]], channel_multiplier=-HD).then_inc(wide_used, 1)
                gp.wait_ge(wide_used, 2)
                gp.affine_select(out=spread[:, :], in_=spread[:, :], compare_op=ALU.is_ge, fill=0.0, base=HD - 1,
                                 pattern=[[-1, C]], channel_multiplier=HD).then_inc(spread_ok, 1)
            for k in range(2 * CH):
                gp.indirect_dma_start(own[:, k // CH, k % CH, :], None, rows,
                                      bass.IndirectOffsetOnAxis(ap=g.sum_idx[:, k:k + 1], axis=0)
                                      ).then_inc(gathered, 16)
            for c in range(TC):
                gp.wait_ge(row_ok, len(jobs) - TC + c + 1)
                gp.indirect_dma_start(table, bass.IndirectOffsetOnAxis(ap=g.chain_idx[:, c:c + 1], axis=0),
                                      row_out[:, c, :], None).then_inc(scattered, 16)
            gp.wait_ge(scattered, 16 * TC)
            gp.wait_ge(gathered, 16 * 2 * CH)


class Steps:

    def __init__(self, eng, sem, per):
        self.eng, self.sem, self.per, self.n, self.base = eng, sem, per, 0, 0

    def round(self, c):
        assert self.n in (0, self.per), self.n
        self.base, self.n = c * self.per, 0

    def at(self):
        return self.base + self.n

    def __call__(self, ins):
        self.n += 1
        ins.then_inc(self.sem, 1)
        self.eng.wait_ge(self.sem, self.base + self.n)


def until(eng, sem, value, passed=None):
    if isinstance(value, int) and value <= 0:
        return
    if passed is None:
        eng.wait_ge(sem, value)
    else:
        hold(eng, sem, value, passed)


def rounds(eng, step, begin, end, ahead):
    stop = (NCH - ahead) // 2
    for c in range(begin, 2):
        step(c // 2, c % 2)
    with eng.Fori(1, stop) as i:
        for u in range(2):
            step(i, u)
    for c in range(2 * stop, end):
        step(c // 2, c % 2)


def at_chunk(i, u, k):
    c = 2 * i + u + k
    return c, i + (u + k) // 2, (u + k) % 2, not isinstance(c, int) or 0 <= c < NCH


def finish_convolution(nc, g, a, own):
    with ExitStack() as ctx:
        sb, pb, sem = scope(nc, ctx)
        idx = sb("d_idx", [P, 2, 2, CH], I32)
        chain = sb("d_chain", [P, 2, CH, W0])
        x_in = sb("d_x", [P, 2, CH, C])
        mid_t = sb("d_mid_t", [P, CH, 2, P])
        pre = sb("d_pre", [P, CH, C])
        raw = sb("d_raw", [P, CH, 6])
        stat = sb("d_stat", [P, CH, 2])
        half = sb("d_half", [P, CH])
        var = sb("d_var", [P, CH])
        rstd = sb("d_rstd", [P, CH])
        x1 = sb("d_x1", [P, 2, CH, C])
        x1_t = sb("d_x1_t", [P, CH, P])
        qvk = sb("d_qvk", [P, 2, CH, 3 * C])
        keys = sb("d_keys", [P, 2, CH, C])
        prod = sb("d_prod", [P, CH, C])
        ps_t = [pb(f"d_ps_t{i}", [P, 4, P]) for i in range(2)]
        ps_o = pb("d_ps_o", [P, 8, C])
        ps_q = [pb(f"d_ps_q{i}", [P, 512]) for i in range(4)]
        x_ok = [sem(f"d_x_in{i}") for i in range(2)]
        chain_ok = [sem(f"d_chain_in{i}") for i in range(2)]
        own_ok = [sem(f"d_own_in{i}") for i in range(2)]
        idx_ok = sem("d_idx_ok")
        k_idx_ok = sem("d_k_idx_ok")
        mid_ok = sem("d_mid")
        t_ok = sem("d_t")
        t_ev = sem("d_tev")
        out_ok = sem("d_out")
        stats_ok = sem("d_stats")
        root_ok = sem("d_root")
        rstd_ok = sem("d_rstdok")
        x1_ok = sem("d_x1ok")
        q_ok = sem("d_q")
        q_ev = sem("d_qev")
        keys_ok = sem("d_keysok")
        self_ok = sem("d_self")
        x1_kept = sem("d_x1_kept")
        qv_out = [sem(f"d_qv_out{i}") for i in range(2)]
        scattered = sem("d_scattered")
        dve = sem("d_dve")
        passed = sem("d_passed")
        block = ctx.enter_context(nc.Block())
        rows = lambda t, c: t[0:NP, :].rearrange("(h p) w -> p h w", p=P)[:, bass.ds(c * CH, CH), :]
        MID = [(0, 4), (4, 8), (8, 12), (12, 14)]
        ONE = [(0, 4), (4, 7)]

        def mid_no(c, n):
            return n if isinstance(c, int) and c == 0 else 6 * c - 2 + n

        def one_no(c, n):
            last = isinstance(c, int) and c == NCH - 1
            return 6 * c + (4 if last else 8) + n

        @block.sync
        def _(sp):
            def step(i, u):
                c, pair, b, there = at_chunk(i, u, 2)
                if there:
                    until(sp, mid_ok, c - 1, passed)
                    sp.dma_start(chain[:, b, :, :], rows(g.chains0, c)).then_inc(chain_ok[b], 16)
                    until(sp, x1_ok, c - 1, passed)
                    sp.dma_start(x_in[:, b, :, :], rows(a["x_rows"], c)).then_inc(x_ok[b], 16)
                c, pair, b, there = at_chunk(i, u, 0)
                if there:
                    until(sp, q_ev, (c + 1) * CH, passed)
                    sp.dma_start(rows(g.qv, c), qvk[:, b, :, 0:2 * C]).then_inc(qv_out[b], 16)
            rounds(sp, step, -2, NCH, 2)
            for b in range(2):
                sp.wait_ge(qv_out[b], 16 * NCH // 2)

        @block.gpsimd
        def _(gp):
            gp.memset(half[:, :], -0.5)

            def gather(i, u):
                c, pair, b, there = at_chunk(i, u, 2)
                if there and not (isinstance(c, int) and c < 2):
                    until(gp, own_ok[b], 16 * CH * (pair - 1), passed)
                    gp.tensor_copy(idx[:, b, 0, :], g.sum_idx[:, bass.ds(c * CH, CH)]).then_inc(idx_ok, 1)
                    until(gp, idx_ok, c - 1, passed)
                    until(gp, t_ok, mid_no(c - 2, 4), passed)
                    for k in range(CH):
                        gp.indirect_dma_start(own[:, b, k, :], None, g.sums0,
                                              bass.IndirectOffsetOnAxis(ap=idx[:, b, 0, k:k + 1], axis=0)
                                              ).then_inc(own_ok[b], 16)

            def root(i, u):
                c, pair, b, there = at_chunk(i, u, 0)
                if there:
                    until(gp, stats_ok, c + 1, passed)
                    gp.tensor_scalar(var[:, :], stat[:, :, 1], EPS, None, ALU.add).then_inc(root_ok, 1)
                    until(gp, root_ok, c + 1, passed)
                    gp.tensor_tensor(rstd[:, :], var[:, :], half[:, :], ALU.pow).then_inc(rstd_ok, 1)

            def scatter(i, u):
                c, pair, b, there = at_chunk(i, u, -1)
                if there:
                    until(gp, scattered, 16 * CH * c, passed)
                    gp.tensor_copy(idx[:, b, 1, :], g.k_idx[:, bass.ds(c * CH, CH)]).then_inc(k_idx_ok, 1)
                    until(gp, k_idx_ok, c + 1, passed)
                    until(gp, keys_ok, c + 1, passed)
                    for k in range(CH):
                        gp.indirect_dma_start(g.k_runs, bass.IndirectOffsetOnAxis(ap=idx[:, b, 1, k:k + 1], axis=0),
                                              keys[:, b, k, :], None).then_inc(scattered, 16)
            def step(i, u):
                gather(i, u)
                root(i, u)
                scatter(i, u)
            rounds(gp, step, -2, NCH + 1, 2)
            gp.wait_ge(scattered, 16 * CH * NCH)

        @block.vector
        def _(v):
            link = Steps(v, dve, CH + 1)

            def keys_of(i, u):
                c, pair, b, there = at_chunk(i, u, -1)
                if there:
                    until(v, q_ev, CH * (c + 1))
                    until(v, scattered, 16 * CH * c)
                    v.tensor_scalar(keys[:, b, :, :], qvk[:, b, :, 2 * C:3 * C], 1.0 / HD ** 0.5, None,
                                    ALU.mult).then_inc(keys_ok, 1)
                    v.wait_ge(keys_ok, c + 1)
                    until(v, self_ok, 2 * c)
                    v.tensor_tensor(prod[:, :, :], keys[:, b, :, :], qvk[:, b, :, 0:C], ALU.mult).then_inc(self_ok, 1)
                    v.wait_ge(self_ok, 2 * c + 1)
                    v.tensor_reduce(g.self_score[:, bass.ds(c * CH, CH), :],
                                    prod[:, :, :].rearrange("p k (h d) -> p k h d", d=HD), AX.X,
                                    ALU.add).then_inc(self_ok, 1)

            def add_chains(i, u):
                c, pair, b, there = at_chunk(i, u, 1)
                if there:
                    until(v, own_ok[b], 16 * CH * pair)
                    until(v, chain_ok[b], 16 * (pair + 1))
                    v.tensor_tensor(own[:, b, :, :], own[:, b, :, :], chain[:, b, :, :], ALU.add).then_inc(mid_ok, 1)

            def finish(i, u):
                c, pair, b, there = at_chunk(i, u, 0)
                if not there:
                    add_chains(i, u)
                    keys_of(i, u)
                    return
                link.round(c)
                until(v, out_ok, c + 1)
                until(v, x_ok[b], 16 * (pair + 1))
                until(v, x1_ok, c)
                for k in range(CH):
                    last = v.scalar_tensor_tensor(pre[:, k, :], ps_o[:, k, :], g.b_scale[:, bass.ds(c * CH + k, 1)],
                                                  x_in[:, b, k, :], ALU.mult, ALU.add)
                link(last)
                for k in range(CH):
                    v.bn_stats(raw[:, k, :], pre[:, k, :]).then_inc(dve, 1)
                    link.n += 1
                hold(v, dve, link.at(), passed)
                for k in range(CH):
                    last = v.bn_aggr(stat[:, k, :], raw[:, k, :])
                last.then_inc(stats_ok, 1)
                add_chains(i, u)
                keys_of(i, u)
                v.wait_ge(rstd_ok, c + 1)
                until(v, x1_kept, c - 1)
                for k in range(CH):
                    last = v.tensor_scalar(x1[:, b, k, :], pre[:, k, :], stat[:, k, 0:1], rstd[:, k:k + 1],
                                           ALU.subtract, ALU.mult)
                last.then_inc(x1_ok, 1)

            rounds(v, finish, -1, NCH + 1, 2)

        @block.scalar
        def _(act):
            def step(i, u):
                c, pair, b, there = at_chunk(i, u, 1)
                if there:
                    until(act, out_ok, c)
                    for n, (lo, hi) in enumerate(MID):
                        act.wait_ge(t_ok, mid_no(c, n) + 1)
                        nc.scalar.activation(mid_t[:, :, :, :].rearrange("p k m n -> p (k m) n")[:, lo:hi, :],
                                             ps_t[n % 2][:, 0:hi - lo, :], ACT.Copy).then_inc(t_ev, 1)
                c, pair, b, there = at_chunk(i, u, 0)
                if there:
                    for n, (lo, hi) in enumerate(ONE):
                        act.wait_ge(t_ok, one_no(c, n) + 1)
                        nc.scalar.activation(x1_t[:, lo:hi, :], ps_t[n % 2][:, 0:hi - lo, :],
                                             ACT.Copy).then_inc(t_ev, 1)
                    nc.scalar.activation(g.x1[:, bass.ds(c * CH, CH), :], x1[:, b, :, :], ACT.Copy).then_inc(x1_kept, 1)
                    until(act, qv_out[b], 16 * pair)
                    until(act, self_ok, 2 * (c - 1))
                    for k in range(CH):
                        act.wait_ge(q_ok, CH * c + k + 1)
                        nc.scalar.activation(qvk[:, b, k, :], ps_q[k % 4][:, 0:3 * C], ACT.Copy).then_inc(q_ev, 1)
            rounds(act, step, -1, NCH, 2)

        @block.tensor
        def _(pe):
            def turn(src, n, lo, hi, no):
                until(pe, t_ev, no - 1)
                for k in range(lo, hi):
                    last = nc.tensor.transpose(ps_t[n % 2][:, k - lo, :], src[:, k, :], g.ident[:, :])
                last.then_inc(t_ok, 1)

            def step(i, u):
                c, pair, b, there = at_chunk(i, u, 1)
                if there:
                    pe.wait_ge(mid_ok, c + 1)
                    for n, (lo, hi) in enumerate(MID):
                        turn(own[:, b, :, :].rearrange("p k (m w) -> p (k m) w", m=2), n, lo, hi, mid_no(c, n))
                    pe.wait_ge(t_ev, mid_no(c, 4))
                    until(pe, stats_ok, c)
                    for k in range(CH):
                        for m in range(2):
                            last = nc.tensor.matmul(ps_o[:, k, :], mid_t[:, k, m, :], g.w_after[:, m, :],
                                                    start=(m == 0), stop=(m == 1))
                    last.then_inc(out_ok, 1)
                c, pair, b, there = at_chunk(i, u, 0)
                if there:
                    pe.wait_ge(x1_ok, c + 1)
                    for n, (lo, hi) in enumerate(ONE):
                        turn(x1[:, b, :, :], n, lo, hi, one_no(c, n))
                    pe.wait_ge(t_ev, one_no(c, 2))
                    for k in range(CH):
                        until(pe, q_ev, CH * c + k + 1 - 4)
                        nc.tensor.matmul(ps_q[k % 4][:, 0:3 * C], x1_t[:, k, :], g.w_qvk[:, :], start=True,
                                         stop=True).then_inc(q_ok, 1)
            rounds(pe, step, -1, NCH, 2)


def edge_attention(nc, g, a):
    with ExitStack() as ctx:
        sb, pb, sem = scope(nc, ctx)
        QT = 4
        NG = T // QT
        U = 8
        ROWS = 8
        idx = sb("e_idx", [P, 2, HALF], I32)
        qv = sb("e_qv", [P, 2, HALF, 2 * C])
        keys = sb("e_keys", [P, 2, HALF, C])
        hot = sb("e_hot", [P, 2, HALF, P])
        hot_t = sb("e_hot_t", [P, 2, QT, P])
        prod = sb("e_prod", [P, QT, C])
        score = sb("e_score", [P, HALF * HEADS])
        reset = sb("e_reset", [P, 2, 2, P])
        fwd = sb("e_fwd", [P, P])
        top = sb("e_top", [P, P])
        diff = sb("e_diff", [P, P])
        top_end = sb("e_top_end", [P, P])
        prob = sb("e_prob", [P, P])
        rhs = sb("e_rhs", [P, 2, HALF, W1])
        out = sb("e_out", [P, 2, QT, W1])
        ps_t = [pb(f"e_ps_t{i}", [P, QT, P]) for i in range(2)]
        ps_k = [pb(f"e_ps_k{i}", [P, QT, C]) for i in range(2)]
        ps_s = pb("e_ps_s", [P, 512])
        ps_b = pb("e_ps_b", [P, 4, P])
        ps_o = [pb(f"e_ps_o{i}", [P, 512]) for i in range(2)]

        idx_in = [sem(f"e_idx_in{i}") for i in range(2)]
        reset_in = [sem(f"e_reset_in{i}") for i in range(2)]
        keys_in = [[sem(f"e_keys_in{i}{q}") for q in range(4)] for i in range(2)]
        gathered = [[sem(f"e_gathered{i}{q}") for q in range(4)] for i in range(2)]
        stored = [sem(f"e_stored{i}") for i in range(2)]
        hot_ok = sem("e_hot_ok")
        turned = sem("e_turned")
        hot_t_ok = sem("e_hot_t_ok")
        keyed = sem("e_keyed")
        multiplied = sem("e_multiplied")
        scored = sem("e_scored")
        score_turned = sem("e_score_turned")
        scans = sem("e_scans")
        diff_ok = sem("e_diff_ok")
        exp_ok = sem("e_exp")
        backed = sem("e_backed")
        copied = sem("e_copied")
        weighted = sem("e_weighted")
        summed = sem("e_summed")
        staged = sem("e_staged")
        cleared = sem("e_cleared")
        passed = sem("e_passed")
        block = ctx.enter_context(nc.Block())
        table = g.sums1[0:EP, :].rearrange("(t r) w -> r t w", r=P)

        def groups(eng, step):
            for u in range(U):
                step(0, u)
            with eng.Fori(1, NG // U - 1) as i:
                for u in range(U):
                    step(i, u)
            for u in range(U):
                step(NG // U - 1, u)

        def early(i, u, n):
            return isinstance(i, int) and U * i + u < n

        def late(i, u, n):
            return isinstance(i, int) and U * i + u >= NG - n

        def ahead(i, u, n):
            return i + (u + n) // U, (u + n) % U

        @block.sync
        def _(sp):
            def load(i, u):
                h = u // 4
                if not early(i, u, U):
                    for q in range(4):
                        hold(sp, gathered[h][q], 16 * QT * i, passed)
                    hold(sp, diff_ok, 2 * i + h - 1, passed)
                    hold(sp, keyed, i * U + u - 4, passed)
                sp.dma_start(idx[:, h, :], a["src_t"][bass.ds(i * 2 + h, 1), :, :].rearrange("o p n -> p (o n)")
                             ).then_inc(idx_in[h], 16)
                sp.dma_start(reset[:, h, :, :],
                             g.resets[bass.ds((i * 2 + h) * HALF, HALF), :, :, :].rearrange("t h m e -> (t h) m e")
                             ).then_inc(reset_in[h], 16)
                for k0 in range(0, HALF, ROWS):
                    t0 = (i * 2 + h) * HALF + k0
                    _, first = nc.values_load_multi_w_load_instructions(
                        g.rank0[0:1, bass.ds(t0, ROWS)], engines=(mybir.EngineType.SP,), min_val=0, max_val=NP)
                    for k, row in enumerate(first, k0):
                        sp.dma_start(keys[:, h, k, :], g.k_runs[bass.ds(row, P), :]).then_inc(keys_in[h][k // QT], 16)

            def step(i, u):
                if u % 4 == 0 and not late(i, u, 4):
                    load(*ahead(i, u, 4))
                if u == 4:
                    sp.dma_start(g.chains1[bass.ds(i * 2 * P, 2 * P), :].rearrange("(h p) w -> p h w", p=P),
                                 g.none1[:, :].unsqueeze(1).broadcast_to([P, 2, W1])).then_inc(cleared, 16)

            load(0, 0)
            groups(sp, step)
            sp.wait_ge(cleared, 16 * NG // U)

        @block.gpsimd
        def _(gp):
            def step(i, u):
                h, q = u // 4, u % 4
                if q == 0:
                    hold(gp, idx_in[h], 16 * (i + 1), passed)
                if not early(i, u, U):
                    hold(gp, weighted, i * U + u - U + 1, passed)
                for k in range(QT):
                    c = QT * q + k
                    gp.indirect_dma_start(qv[:, h, c, :], None, g.qv,
                                          bass.IndirectOffsetOnAxis(ap=idx[:, h, c:c + 1], axis=0)
                                          ).then_inc(gathered[h][q], 16)
            groups(gp, step)

        @block.scalar
        def _(act):
            def copy_hot(i, u):
                j = i * U + u
                act.wait_ge(turned, j + 1)
                if not early(i, u, 2):
                    act.wait_ge(keyed, j - 1)
                nc.scalar.activation(hot_t[:, u % 2, :, :], ps_t[u % 2][:, :, :], ACT.Copy).then_inc(hot_t_ok, 1)

            def copy_back(i, u):
                h, n = u // 4, 2 * i + u // 4
                act.wait_ge(backed, n + 1)
                if not early(i, u, U):
                    act.wait_ge(summed, i * U + u - 4)
                nc.scalar.activation(rhs[:, h, :, C:W1].rearrange("p t (m x) -> p m t x", m=2),
                                     ps_b[:, 0:2, :].rearrange("p m (t x) -> p m t x", x=HEADS),
                                     ACT.Copy).then_inc(copied, 1)

            def stage(i, u):
                j = i * U + u
                act.wait_ge(summed, j + 1)
                if not early(i, u, 2):
                    act.wait_ge(stored[u % 2], 16 * (4 * i + (u - 2) // 2 + 1))
                for m in range(2):
                    last = nc.scalar.activation(out[:, u % 2, 2 * m:2 * m + 2, :],
                                                ps_o[m][:, 0:2 * W1].rearrange("p (k w) -> p k w", k=2), ACT.Copy)
                last.then_inc(staged, 1)

            def store(i, u):
                j = i * U + u
                act.wait_ge(staged, j + 1)
                act.dma_start(table[:, bass.ds(j * QT, QT), :], out[:, u % 2, :, :]).then_inc(stored[u % 2], 16)

            def step(i, u):
                if not late(i, u, 1):
                    copy_hot(*ahead(i, u, 1))
                if not early(i, u, 4):
                    if u % 4 == 0:
                        copy_back(*ahead(i, u, -4))
                    if not early(i, u, 5):
                        store(*ahead(i, u, -5))
                    stage(*ahead(i, u, -4))
                if u % 4 == 3:
                    n = 2 * i + u // 4
                    act.wait_ge(diff_ok, n + 1)
                    if not early(i, u, 4):
                        act.wait_ge(backed, n)
                    nc.scalar.activation(prob[:, :], diff[:, :], ACT.Exp).then_inc(exp_ok, 1)

            copy_hot(0, 0)
            groups(act, step)
            copy_back(NG // U - 1, 4)
            for u in range(4, U):
                store(NG // U - 1, u - 1)
                stage(NG // U - 1, u)
            store(NG // U - 1, U - 1)
            for b in range(2):
                act.wait_ge(stored[b], 16 * NG // 2)

        @block.vector
        def _(v):
            def one_hot(i, u):
                j, h, q = i * U + u, u // 4, u % 4
                if not early(i, u, U):
                    v.wait_ge(summed, j - U + 1)
                for k in range(QT):
                    last = v.tensor_scalar(hot[:, h, QT * q + k, :], g.column[:, :],
                                           g.rel[:, bass.ds(j * QT + k, 1)], None, ALU.is_equal)
                last.then_inc(hot_ok, 1)

            def weigh(i, u):
                h, q = u // 4, u % 4
                ts = slice(QT * q, QT * q + QT)
                if q == 0:
                    v.wait_ge(copied, 2 * i + h + 1)
                v.tensor_tensor(rhs[:, h, ts, 0:C].rearrange("p t (x d) -> p t x d", d=HD),
                                qv[:, h, ts, C:2 * C].rearrange("p t (x d) -> p t x d", d=HD),
                                rhs[:, h, ts, C:C + HEADS].unsqueeze(3).broadcast_to([P, QT, HEADS, HD]),
                                ALU.mult).then_inc(weighted, 1)

            def scores(i, u):
                j, h, q = i * U + u, u // 4, u % 4
                v.wait_ge(gathered[h][q], 16 * QT * (i + 1))
                v.wait_ge(keyed, j + 1)
                if not early(i, u, 1):
                    v.wait_ge(scored, j)
                v.tensor_tensor(prod[:, :, :], ps_k[u % 2][:, :, :], qv[:, h, QT * q:QT * q + QT, 0:C],
                                ALU.mult).then_inc(multiplied, 1)
                v.wait_ge(multiplied, j + 1)
                if q == 0 and not early(i, u, 4):
                    v.wait_ge(score_turned, 2 * i + h)
                v.tensor_reduce(score[:, QT * HEADS * q:QT * HEADS * (q + 1)],
                                prod[:, :, :].rearrange("p t (x d) -> p t x d", d=HD), AX.X,
                                ALU.add).then_inc(scored, 1)

            def maxima(i, u):
                h = u // 4
                n = 2 * i + h
                v.wait_ge(score_turned, n + 1)
                v.wait_ge(reset_in[h], 16 * (i + 1))
                v.tensor_tensor_scan(fwd[:, :], reset[:, h, 0, :], ps_s[:, 0:P], -BIG, ALU.add,
                                     ALU.max).then_inc(scans, 1)
                v.wait_ge(scans, 3 * n + 1)
                if not early(i, u, 4):
                    v.wait_ge(backed, n)
                v.tensor_tensor_scan(top[:, ::-1], reset[:, h, 1, ::-1], fwd[:, ::-1], -BIG, ALU.add,
                                     ALU.max).then_inc(scans, 1)
                v.wait_ge(scans, 3 * n + 2)
                v.scalar_tensor_tensor(top_end[:, :], reset[:, h, 1, :], 0.0, top[:, :], ALU.is_lt,
                                       ALU.mult).then_inc(scans, 1)
                v.tensor_tensor(diff[:, :], ps_s[:, 0:P], top[:, :], ALU.subtract).then_inc(diff_ok, 1)

            def step(i, u):
                q = u % 4
                if q != 3 and not late(i, u, 2):
                    one_hot(*ahead(i, u, 2))
                if q < 2 and not early(i, u, 4):
                    bi, bu = ahead(i, u, -4)
                    weigh(bi, bu + q)
                    weigh(bi, bu + q + 1)
                scores(i, u)
                if q == 3:
                    if not late(i, u, 2):
                        one_hot(*ahead(i, u, 2))
                    maxima(i, u)

            one_hot(0, 0)
            one_hot(0, 1)
            groups(v, step)
            for u in range(4, U):
                weigh(NG // U - 1, u)

        @block.tensor
        def _(pe):
            def turn(i, u):
                j, h, q = i * U + u, u // 4, u % 4
                pe.wait_ge(hot_ok, j + 1)
                if not early(i, u, 2):
                    pe.wait_ge(hot_t_ok, j - 1)
                for k in range(QT):
                    last = nc.tensor.transpose(ps_t[u % 2][:, k, :], hot[:, h, QT * q + k, :], g.ident[:, :])
                last.then_inc(turned, 1)

            def spread_keys(i, u):
                j, h, q = i * U + u, u // 4, u % 4
                pe.wait_ge(hot_t_ok, j + 1)
                pe.wait_ge(keys_in[h][q], 16 * QT * (i + 1))
                if not early(i, u, 2):
                    pe.wait_ge(multiplied, j - 1)
                for k in range(QT):
                    last = nc.tensor.matmul(ps_k[u % 2][:, k, :], hot_t[:, u % 2, k, :],
                                            keys[:, h, QT * q + k, :], start=True, stop=True)
                last.then_inc(keyed, 1)

            def back(i, u):
                n = 2 * i + u // 4
                pe.wait_ge(exp_ok, n + 1)
                if not early(i, u, 4):
                    pe.wait_ge(copied, n)
                nc.tensor.transpose(ps_b[:, 0, :], prob[:, :], g.ident[:, :])
                nc.tensor.transpose(ps_b[:, 1, :], top_end[:, :], g.ident[:, :]).then_inc(backed, 1)

            def sums(i, u):
                j, h, q = i * U + u, u // 4, u % 4
                pe.wait_ge(weighted, j + 1)
                if not early(i, u, 1):
                    pe.wait_ge(staged, j)
                for k in range(QT):
                    last = nc.tensor.matmul(ps_o[k // 2][:, W1 * (k % 2):W1 * (k % 2) + W1],
                                            hot[:, h, QT * q + k, :], rhs[:, h, QT * q + k, :],
                                            start=True, stop=True)
                last.then_inc(summed, 1)

            def step(i, u):
                if not late(i, u, 1):
                    turn(*ahead(i, u, 1))
                spread_keys(i, u)
                if not early(i, u, 4):
                    if u % 4 == 0:
                        back(*ahead(i, u, -4))
                    sums(*ahead(i, u, -4))
                if u % 4 == 3:
                    n = 2 * i + u // 4
                    pe.wait_ge(scored, i * U + u + 1)
                    if not early(i, u, 4):
                        pe.wait_ge(diff_ok, n)
                    nc.tensor.transpose(ps_s[:, 0:P], score[:, :], g.ident[:, :]).then_inc(score_turned, 1)

            turn(0, 0)
            groups(pe, step)
            back(NG // U - 1, 4)
            for u in range(4, U):
                sums(NG // U - 1, u)


def finish_attention(nc, g, a, own, out):
    with ExitStack() as ctx:
        sb, pb, sem = scope(nc, ctx)
        HH = CH * P // 2
        HID_STEPS = 2 * FF // P
        wo = sb("f_wo", [P, C])
        wf1 = sb("f_wf1", [P, FF])
        wf2 = sb("f_wf2", [P, FF // P, C])
        bf1 = sb("f_bf1", [P, FF // P])
        vecs = sb("f_vecs", [P, 6, C])
        idx = sb("f_idx", [P, 2, CH], I32)
        chain = sb("f_chain", [P, 2, CH, W1])
        values = sb("f_values", [P, 2, CH, C])
        top = sb("f_top", [P, CH, HEADS])
        part = sb("f_part", [P, 3, CH, HEADS])
        den = sb("f_den", [P, 2, CH, HEADS])
        acc = sb("f_acc", [P, 2, 3, CH, C])
        acc_t = sb("f_acc_t", [P, CH, P])
        x1_bo = sb("f_x1_bo", [P, 2, CH, C])
        x1_b2 = sb("f_x1_b2", [P, 2, CH, C])
        pre = [sb(f"f_pre{i}", [P, CH, C]) for i in range(3)]
        y1 = sb("f_y1", [P, 2, CH, C])
        y1_bf = sb("f_y1_bf", [P, 2, CH, C])
        y1_t = sb("f_y1_t", [P, CH * P])
        hid = sb("f_hid", [P, FF // P, CH * P])
        y2 = sb("f_y2", [P, CH, C])
        res = sb("f_res", [P, 2, CH, C])
        half = sb("f_half", [P, CH])
        raw = [sb(f"f_raw{i}", [P, CH, 6]) for i in range(3)]
        stat = [sb(f"f_stat{i}", [P, CH, 2]) for i in range(3)]
        var = [sb(f"f_var{i}", [P, CH]) for i in range(3)]
        rstd = [sb(f"f_rstd{i}", [P, CH]) for i in range(3)]
        shift = [sb(f"f_shift{i}", [P, 2, CH]) for i in range(3)]
        ps_t = [pb(f"f_ps_t{i}", [P, 4, P]) for i in range(2)]
        ps_o = pb("f_ps_o", [P, 8, C])
        ps_r = pb("f_ps_r", [P, 8, C])
        ps_h = [pb(f"f_ps_h{i}", [P, 512]) for i in range(2)]
        w_in = sem("f_w_in")
        chain_ok = [sem(f"f_chain_in{i}") for i in range(2)]
        values_ok = [sem(f"f_values_in{i}") for i in range(2)]
        own_ok = [sem(f"f_own_in{i}") for i in range(2)]
        idx_ok = sem("f_idx_ok")
        diff_ok = sem("f_diff")
        part_ok = sem("f_part_ok")
        acc_ok = sem("f_acc_ok")
        acc_turned = sem("f_acc_turned")
        acc_t_ok = sem("f_acc_t_ok")
        o_ok = sem("f_o")
        x1_bo_ok = sem("f_x1_bo_ok")
        x1_b2_ok = sem("f_x1_b2_ok")
        stats_ok = [sem(f"f_stats{i}") for i in range(3)]
        root_ok = [sem(f"f_root{i}") for i in range(3)]
        rstd_ok = [sem(f"f_rstdok{i}") for i in range(3)]
        y1_in = sem("f_y1in")
        y1_ok = sem("f_y1ok")
        y1_bf_ok = sem("f_y1_bf_ok")
        y1_turned = sem("f_y1_turned")
        y1_t_ok = sem("f_y1_t_ok")
        h_ok = sem("f_h")
        hid_ok = sem("f_hid_ok")
        ffn_ok = sem("f_ffn")
        y2_ok = sem("f_y2ok")
        res_ok = sem("f_resok")
        stored = sem("f_stored")
        join = sem("f_join")
        norm = [sem(f"f_norm{i}") for i in range(3)]
        passed = sem("f_passed")
        block = ctx.enter_context(nc.Block())
        rows = lambda t, c: t[0:NP, :].rearrange("(h p) w -> p h w", p=P)[:, bass.ds(c * CH, CH), :]
        ONE = [(0, 4), (4, 7)]
        vec = lambda n: vecs[:, n:n + 1, :].broadcast_to([P, CH, C])
        wide = lambda t: t.unsqueeze(3).broadcast_to([P, CH, HEADS, HD])
        by_head = lambda t: t.rearrange("p k (x d) -> p k x d", d=HD)
        x1_of = lambda c: g.x1[:, bass.ds(c * CH, CH), :]
        first, last = -3, NCH + 1

        @block.sync
        def _(sp):
            sp.dma_start(wo[:, :], a["wo"]).then_inc(w_in, 16)
            sp.dma_start(wf1[:, :], a["wf1"]).then_inc(w_in, 16)
            sp.dma_start(wf2[:, :, :], a["wf2"].rearrange("(c p) n -> p c n", p=P)).then_inc(w_in, 16)
            sp.dma_start(bf1[:, :], a["bf1_t"]).then_inc(w_in, 16)
            sp.dma_start(vecs[:, :, :], a["vecs"].unsqueeze(0).broadcast_to([P, 6, C])).then_inc(w_in, 16)

            def step(i, u):
                c, pair, b, there = at_chunk(i, u, 3)
                if there:
                    until(sp, acc_ok, c - 1, passed)
                    sp.dma_start(chain[:, b, :, :], rows(g.chains1, c)).then_inc(chain_ok[b], 16)
                    sp.dma_start(values[:, b, :, :], rows(g.qv, c)[:, :, C:2 * C]).then_inc(values_ok[b], 16)
                c, pair, b, there = at_chunk(i, u, -1)
                if there:
                    until(sp, res_ok, c + 1, passed)
                    sp.dma_start(rows(out, c), res[:, b, :, :]).then_inc(stored, 16)
            rounds(sp, step, first, last, 3)
            sp.wait_ge(stored, 16 * NCH)

        @block.gpsimd
        def _(gp):
            gp.memset(half[:, :], -0.5)
            gp.wait_ge(w_in, 80)

            def root(n, i, u, k):
                c, pair, b, there = at_chunk(i, u, k)
                if there:
                    until(gp, stats_ok[n], c + 1, passed)
                    gp.tensor_scalar(shift[n][:, 0, :], stat[n][:, :, 0], -1.0, None, ALU.mult)
                    gp.tensor_scalar(var[n][:, :], stat[n][:, :, 1], EPS, None, ALU.add).then_inc(root_ok[n], 1)
                    until(gp, root_ok[n], 2 * c + 1, passed)
                    gp.tensor_tensor(rstd[n][:, :], var[n][:, :], half[:, :], ALU.pow).then_inc(root_ok[n], 1)
                    until(gp, root_ok[n], 2 * c + 2, passed)
                    gp.tensor_tensor(shift[n][:, 1, :], shift[n][:, 0, :], rstd[n][:, :],
                                     ALU.mult).then_inc(rstd_ok[n], 1)

            def step(i, u):
                root(1, i, u, -1)
                c, pair, b, there = at_chunk(i, u, 3)
                if there and not (isinstance(c, int) and c < 2):
                    until(gp, own_ok[b], 16 * CH * (pair - 1), passed)
                    gp.tensor_copy(idx[:, b, :], g.sum_idx[:, bass.ds(c * CH, CH)]).then_inc(idx_ok, 1)
                    until(gp, idx_ok, c - 1, passed)
                    until(gp, acc_ok, c - 1, passed)
                    for k in range(CH):
                        gp.indirect_dma_start(own[:, b, k, :], None, g.sums1,
                                              bass.IndirectOffsetOnAxis(ap=idx[:, b, k:k + 1], axis=0)
                                              ).then_inc(own_ok[b], 16)
                root(0, i, u, 1)
                root(2, i, u, -1)
                c, pair, b, there = at_chunk(i, u, 2)
                if there:
                    until(gp, stats_ok[0], c - 1, passed)
                    gp.tensor_tensor(x1_bo[:, b, :, :], x1_of(c), vec(0), ALU.add).then_inc(x1_bo_ok, 1)
                c, pair, b, there = at_chunk(i, u, 0)
                if there:
                    until(gp, stats_ok[2], c - 1, passed)
                    gp.tensor_tensor(x1_b2[:, b, :, :], x1_of(c), vec(5), ALU.add).then_inc(x1_b2_ok, 1)
                c, pair, b, there = at_chunk(i, u, 1)
                if there:
                    until(gp, y1_ok, c + 1, passed)
                    until(gp, stats_ok[1], c - 1, passed)
                    gp.tensor_tensor(y1_bf[:, b, :, :], y1[:, b, :, :], vec(1), ALU.add).then_inc(y1_bf_ok, 1)
            rounds(gp, step, first, last, 3)

        @block.vector
        def _(v):
            joined = Steps(v, join, 5)
            weighed = Steps(v, diff_ok, 3)
            normed = [Steps(v, norm[0], CH + 2), Steps(v, norm[1], CH + 1), Steps(v, norm[2], CH + 2)]

            def stats(n, ready):
                for k in range(CH):
                    v.bn_stats(raw[n][:, k, :], pre[n][:, k, :]).then_inc(norm[n], 1)
                    normed[n].n += 1
                hold(v, norm[n], normed[n].at(), passed)
                for k in range(CH):
                    last_one = v.bn_aggr(stat[n][:, k, :], raw[n][:, k, :])
                last_one.then_inc(stats_ok[n], 1)

            def second_input(i, u):
                c, pair, b, there = at_chunk(i, u, -1)
                if there:
                    normed[1].round(c)
                    until(v, ffn_ok, c + 1)
                    until(v, y1_bf_ok, c + 1)
                    normed[1](v.tensor_tensor(pre[1][:, :, :], ps_r[:, 0:CH, :], y1_bf[:, b, :, :], ALU.add))
                    stats(1, c)

            def joins(i, u):
                c, pair, b, there = at_chunk(i, u, 2)
                if there:
                    joined.round(c)
                    until(v, part_ok, c + 1)
                    v.tensor_tensor(den[:, 0, :, :], own[:, b, :, C:C + HEADS], part[:, 0, :, :], ALU.mult)
                    joined(v.tensor_tensor(den[:, 1, :, :], chain[:, b, :, C:C + HEADS], part[:, 1, :, :], ALU.mult))
                    joined(v.tensor_tensor(den[:, 0, :, :], den[:, 0, :, :], den[:, 1, :, :], ALU.add))
                    joined(v.scalar_tensor_tensor(den[:, 0, :, :], den[:, 0, :, :], 1e-8, part[:, 2, :, :],
                                                  ALU.add, ALU.add))
                    joined(v.reciprocal(den[:, 0, :, :], den[:, 0, :, :]))
                    joined(v.tensor_tensor(part[:, :, :, :], part[:, :, :, :],
                                           den[:, 0:1, :, :].broadcast_to([P, 3, CH, HEADS]), ALU.mult))
                    until(v, values_ok[b], 16 * (pair + 1))
                    until(v, o_ok, c - 1)
                    for m, src in enumerate((own[:, b, :, 0:C], chain[:, b, :, 0:C], values[:, b, :, :])):
                        one = v.tensor_tensor(by_head(acc[:, b, m, :, :]), by_head(src), wide(part[:, m, :, :]),
                                              ALU.mult)
                    one.then_inc(acc_ok, 1)

            def third_input(i, u):
                c, pair, b, there = at_chunk(i, u, -1)
                if there:
                    normed[2].round(c)
                    until(v, y2_ok, c + 1)
                    normed[2](v.tensor_tensor(y2[:, :, :], y2[:, :, :], vec(4), ALU.mult))
                    until(v, res_ok, c)
                    until(v, x1_b2_ok, c + 1)
                    normed[2](v.tensor_tensor(pre[2][:, :, :], y2[:, :, :], x1_b2[:, b, :, :], ALU.add))
                    stats(2, c)

            def first_input(i, u):
                c, pair, b, there = at_chunk(i, u, 1)
                if there:
                    normed[0].round(c)
                    until(v, o_ok, c + 1)
                    until(v, x1_bo_ok, c + 1)
                    normed[0](v.tensor_tensor(pre[0][:, :, :], ps_o[:, 0:CH, :], x1_bo[:, b, :, :], ALU.add))
                    stats(0, c)

            def weighs(i, u):
                c, pair, b, there = at_chunk(i, u, 3)
                if there:
                    weighed.round(c)
                    until(v, own_ok[b], 16 * CH * pair)
                    until(v, chain_ok[b], 16 * (pair + 1))
                    self_s = g.self_score[:, bass.ds(c * CH, CH), :]
                    own_m, chain_m = own[:, b, :, C + HEADS:W1], chain[:, b, :, C + HEADS:W1]
                    weighed(v.tensor_tensor(top[:, :, :], own_m, chain_m, ALU.max))
                    weighed(v.tensor_tensor(top[:, :, :], top[:, :, :], self_s, ALU.max))
                    v.tensor_tensor(part[:, 0, :, :], own_m, top[:, :, :], ALU.subtract)
                    v.tensor_tensor(part[:, 1, :, :], chain_m, top[:, :, :], ALU.subtract)
                    weighed(v.tensor_tensor(part[:, 2, :, :], self_s, top[:, :, :], ALU.subtract))

            def first_norm(i, u):
                c, pair, b, there = at_chunk(i, u, 1)
                if there:
                    y1_v = y1[:, b, :, :]
                    v.wait_ge(y1_in, c + 1)
                    normed[0](v.tensor_tensor(y1_v, y1_v, vec(2), ALU.mult))
                    v.tensor_tensor(y1_v, y1_v, vec(3), ALU.add).then_inc(y1_ok, 1)

            def step(i, u):
                second_input(i, u)
                joins(i, u)
                first_input(i, u)
                third_input(i, u)
                weighs(i, u)
                first_norm(i, u)
            v.wait_ge(w_in, 80)
            rounds(v, step, first, last, 3)

        @block.scalar
        def _(act):
            act.wait_ge(w_in, 80)

            def scaled(n, dst, c, done, ks=range(CH)):
                if 0 in ks:
                    act.wait_ge(rstd_ok[n], c + 1)
                for k in ks:
                    one = nc.scalar.activation(dst(k), pre[n][:, k, :], ACT.Identity,
                                               bias=shift[n][:, 1, k:k + 1], scale=rstd[n][:, k:k + 1])
                if CH - 1 in ks:
                    one.then_inc(done, 1)

            def step(i, u):
                c, pair, b, there = at_chunk(i, u, 1)
                if there:
                    until(act, o_ok, c)
                    for n, (lo, hi) in enumerate(ONE):
                        act.wait_ge(acc_turned, 2 * c + n + 1)
                        nc.scalar.activation(acc_t[:, lo:hi, :], ps_t[n][:, 0:hi - lo, :],
                                             ACT.Copy).then_inc(acc_t_ok, 1)
                c, pair, b, there = at_chunk(i, u, 0)
                if there:
                    until(act, ffn_ok, c)
                    for n, (lo, hi) in enumerate(ONE):
                        act.wait_ge(y1_turned, 2 * c + n + 1)
                        nc.scalar.activation(y1_t[:, lo * P:hi * P].rearrange("p (k n) -> p k n", n=P),
                                             ps_t[n][:, 0:hi - lo, :], ACT.Copy).then_inc(y1_t_ok, 1)
                before, _, _, second = at_chunk(i, u, -1)
                c, pair, b, there = at_chunk(i, u, 0)
                for n in range(HID_STEPS):
                    if there:
                        act.wait_ge(h_ok, HID_STEPS * c + n + 1)
                        nc.scalar.activation(hid[:, n // 2, HH * (n % 2):HH * (n % 2) + HH], ps_h[n % 2][:, 0:HH],
                                             ACT.Gelu, bias=bf1[:, n // 2:n // 2 + 1]).then_inc(hid_ok, 1)
                    if second and n < (CH + 1) // 2:
                        if n == 0:
                            until(act, stats_ok[2], before)
                        scaled(1, lambda k: y2[:, k, :], before, y2_ok, range(2 * n, min(2 * n + 2, CH)))
                c, pair, b, there = at_chunk(i, u, 1)
                if there:
                    until(act, ffn_ok, c - 1)
                    until(act, y1_bf_ok, c - 1)
                    scaled(0, lambda k: y1[:, b, k, :], c, y1_in)
                c, pair, b, there = at_chunk(i, u, 3)
                if there:
                    act.wait_ge(diff_ok, 3 * c + 3)
                    nc.scalar.activation(part[:, :, :, :], part[:, :, :, :], ACT.Exp).then_inc(part_ok, 1)
                c, pair, b, there = at_chunk(i, u, -1)
                if there:
                    until(act, stored, 16 * c)
                    scaled(2, lambda k: res[:, b, k, :], c, res_ok)
            rounds(act, step, first, last, 3)

        @block.tensor
        def _(pe):
            pe.wait_ge(w_in, 80)

            def turn(src, n, turned):
                lo, hi = ONE[n]
                for k in range(lo, hi):
                    one = nc.tensor.transpose(ps_t[n][:, k - lo, :], src[:, k, :], g.ident[:, :])
                one.then_inc(turned, 1)

            def step(i, u):
                c, pair, b, there = at_chunk(i, u, 1)
                if there:
                    pe.wait_ge(acc_ok, c + 1)
                    for n in range(2):
                        until(pe, y1_t_ok, 2 * c + n - 3)
                        lo, hi = ONE[n]
                        for k in range(lo, hi):
                            for m in range(3):
                                one = nc.tensor.matmul(ps_t[n][:, k - lo, :], acc[:, b, m, k, :], g.ident[:, :],
                                                       start=(m == 0), stop=(m == 2))
                        one.then_inc(acc_turned, 1)
                c, pair, b, there = at_chunk(i, u, 0)
                if there:
                    pe.wait_ge(y1_ok, c + 1)
                    for n in range(2):
                        if not isinstance(c, int) or c + 1 < NCH:
                            pe.wait_ge(acc_t_ok, 2 * c + n + 3)
                        turn(y1[:, b, :, :], n, y1_turned)
                c, pair, b, there = at_chunk(i, u, 1)
                if there:
                    pe.wait_ge(acc_t_ok, 2 * c + 2)
                    until(pe, stats_ok[0], c)
                    for k in range(CH):
                        one = nc.tensor.matmul(ps_o[:, k, :], acc_t[:, k, :], wo[:, :], start=True, stop=True)
                    one.then_inc(o_ok, 1)
                c, pair, b, there = at_chunk(i, u, 0)
                if there:
                    pe.wait_ge(y1_t_ok, 2 * c + 2)
                    for n in range(HID_STEPS):
                        until(pe, hid_ok, HID_STEPS * c + n - 1)
                        nc.tensor.matmul(ps_h[n % 2][:, 0:HH], wf1[:, P * (n // 2):P * (n // 2) + P],
                                         y1_t[:, HH * (n % 2):HH * (n % 2) + HH], start=True,
                                         stop=True).then_inc(h_ok, 1)
                    pe.wait_ge(hid_ok, HID_STEPS * (c + 1))
                    until(pe, stats_ok[1], c)
                    for k in range(CH):
                        for m in range(FF // P):
                            one = nc.tensor.matmul(ps_r[:, k, :], hid[:, m, k * P:(k + 1) * P], wf2[:, m, :],
                                                   start=(m == 0), stop=(m == FF // P - 1))
                    one.then_inc(ffn_ok, 1)
            rounds(pe, step, first, last, 3)


def program(nc, a, out):
    g = Shared()

    def dram(name, shape, dt=F32):
        return nc.dram_tensor("table_" + name, shape, dt, kind="Internal").ap()

    g.aux = dram("aux", [T, AUX], I32)
    g.resets = dram("resets", [T, HEADS, 2, P])
    g.keep = dram("keep", [T])
    g.f0 = dram("f0", [NP, C])
    g.qv = dram("qv", [NP, 2 * C])
    g.k_runs = dram("k_runs", [NP + P, C])
    g.sums0 = dram("sums0", [EP + P, W0])
    g.sums1 = dram("sums1", [EP + P, W1])
    g.chains0 = dram("chains0", [NP + T, W0])
    g.chains1 = dram("chains1", [NP + T, W1])
    with ExitStack() as ctx:
        sb, _, _ = scope(nc, ctx)
        g.rel = sb("rel", [P, T])
        g.column = sb("column", [P, P])
        g.ident = sb("ident", [P, P])
        g.k_idx = sb("k_idx", [P, NB], I32)
        g.sum_idx = sb("sum_idx", [P, NB], I32)
        g.chain_idx = sb("chain_idx", [TP, TC], I32)
        g.b_scale = sb("b_scale", [P, NB])
        g.none0 = sb("none0", [P, W0])
        g.none1 = sb("none1", [P, W1])
        g.w_after_in = sb("w_after_in", [P, 2, MUL])
        g.w_after = sb("w_after", [P, 2, C])
        g.rank0 = sb("rank0", [1, T], I32)
        g.self_score = sb("self_score", [P, NB, HEADS])
        g.w_qvk = sb("w_qvk", [P, 3 * C])
        with ExitStack() as first:
            sb1 = lambda name, shape: first.enter_context(nc.sbuf_tensor(name, shape, F32))
            g.y = sb1("y", [P, T, 4])
            g.reset = sb1("reset", [TP, TC, 2, P])
            g.w_node = sb1("w_node", [P, C])
            g.w_hidden = sb1("w_hidden", [P, C])
            g.w_mix = sb1("w_mix", [P, 2, C])
            prepare(nc, g, a)
            edge_convolution(nc, g, a)
        g.x1 = sb("x1_all", [P, NB, C])
        with nc.sbuf_tensor("own0", [P, 2, CH, W0], F32) as own:
            chain_sums(nc, g, g.sums0, g.chains0, W0, "cc_", False, own)
            finish_convolution(nc, g, a, own)
        edge_attention(nc, g, a)
        with nc.sbuf_tensor("own1", [P, 2, CH, W1], F32) as own:
            chain_sums(nc, g, g.sums1, g.chains1, W1, "ec_", True, own)
            finish_attention(nc, g, a, own, out)


def layout(inputs):
    import numpy as np

    x = np.asarray(inputs["x"])
    pad_nodes = lambda v: np.concatenate([v, np.zeros((NP - N_NODES,) + v.shape[1:], v.dtype)])
    pad_edges = lambda v, fill: np.concatenate([v, np.full((EP - N_EDGES,) + v.shape[1:], fill, v.dtype)])
    by_block = lambda v: np.ascontiguousarray(pad_nodes(np.asarray(v))[:, 0].reshape(NB, P).T)
    dst = pad_edges(np.asarray(inputs["dst"]), NP - 1)
    flat = np.concatenate([np.full(LEAD, -1, np.int32), dst, np.full(LEAD, -2, np.int32)]).astype(np.int32)
    by_tile = lambda v: np.ascontiguousarray(v.reshape(T, P).T)
    at = lambda off: flat[LEAD + off:LEAD + off + EP:P].reshape(TP, TC)
    e8 = pad_edges(np.asarray(inputs["edge_attr_8"]), 0)
    e8 = e8.reshape(NH, 4, 2, 2, P, 8).transpose(0, 1, 3, 5, 2, 4).reshape(NH, 4, 16, 2 * P)
    e8 = np.concatenate([e8, np.zeros_like(e8)], axis=2).reshape(NH, P, 2 * P)
    w = lambda k: np.asarray(inputs[k])
    return {
        "x_rows": pad_nodes(x), "x_t": pad_nodes(x).T,
        "dst_flat": flat, "dst_t": by_tile(dst), "prev_t": by_tile(flat[LEAD - 1:LEAD - 1 + EP]),
        "around": np.stack([at(-P), at(-P - 1), at(P)], axis=1),
        "src_t": pad_edges(w("src"), 0).reshape(NH, HALF, P).transpose(0, 2, 1),
        "edge4": pad_edges(w("edge_attr_4"), 0).reshape(T, P, 4).transpose(1, 0, 2),
        "edge8_t": e8, "a_in": by_block(w("node_vec1")), "b_in": by_block(w("node_vec1_n2")),
        "w1_s": w("L0_gnn_w1_s"), "w1_v": w("L0_gnn_w1_v"), "wfc1": w("L0_gnn_Wfc1"), "wfc2": w("L0_gnn_Wfc2"),
        "w2_s": w("L0_gnn_w2_s"), "w2_v": w("L0_gnn_w2_v"),
        "wq": w("L1_gnn_Wq"), "wk": w("L1_gnn_Wk"), "wv": w("L1_gnn_Wv"), "wo": w("L1_gnn_Wo"),
        "wf1": w("L1_gnn_Wf1"), "wf2": w("L1_gnn_Wf2"), "bf1_t": w("L1_gnn_bf1").reshape(FF // P, P).T,
        "vecs": np.stack([w("L1_gnn_" + k) for k in ("bo", "bf2", "g1", "b1", "g2", "b2")]),
    }


def kernel(**inputs):
    import numpy as np
    import concourse.bacc as bacc
    from concourse.bass_utils import run_bass_kernel_spmd

    nc = bacc.Bacc("TRN2", target_bir_lowering=False, num_devices=1)
    arrays = {}
    drams = {}
    for name, v in layout(inputs).items():
        v = np.ascontiguousarray(v)
        arrays["in_" + name] = v
        drams[name] = nc.dram_tensor("in_" + name, v.shape, mybir.dt.from_np(v.dtype),
                                     kind="ExternalInput").ap()
    out = nc.dram_tensor("out_0", [NP, C], F32, kind="ExternalOutput").ap()
    program(nc, drams, out)
    r = run_bass_kernel_spmd(nc, [arrays], core_ids=[0])
    return r.results[0]["out_0"][0:N_NODES]
```
